# Optimizing a Trainium2 kernel written in Bass

```python
import numpy as np
import jax
import jax.numpy as jnp

def _softmax(x, axis=-1):
    return jax.nn.softmax(x, axis=axis)
def _gelu(x):
    return jax.nn.gelu(x, approximate=True)
def _silu(x):
    return jax.nn.silu(x)
def _sigmoid(x):
    return jax.nn.sigmoid(x)
def _layernorm(x, axis=-1, eps=1e-5):
    m = jnp.mean(x, axis=axis, keepdims=True)
    v = jnp.var(x, axis=axis, keepdims=True)
    return (x - m) / jnp.sqrt(v + eps)
def _scatter_add(tgt, idx, src, axis=0):
    return tgt.at[idx].add(src)
def _segment_sum(src, seg, n):
    return jax.ops.segment_sum(src, seg, n)

kernel_name = 'mk_conv_preact_d2_conv_nchw32_08e198'

def setup_inputs(seed: int = 0):
    np.random.seed(seed)
    _w = jnp.asarray
    def _rec_inputs():
        import jax
        import jax.numpy as jnp
        _gk = jax.random.key(seed)
        x = -7.109e-05 + 0.9999 * jax.random.normal(jax.random.fold_in(_gk, 1), (8, 32, 512, 512), jnp.float32)
        return x
    x = _rec_inputs()
    def _L0_conv_setup():
        import jax, jax.numpy as jnp
        import numpy as np
        from jax import lax
        PS = 2
        DN = ('NCHW', 'OIHW', 'NCHW')
        key = jax.random.key(seed)
        ks = jax.random.split(key, 7)
        B, C, H, W = (8, 32, 512, 512)
        return {'x': jax.random.normal(ks[0], (B, C, H, W), dtype=jnp.float32), 'mlp_w': jax.random.normal(ks[1], (1, 1), dtype=jnp.float32), 'mlp_b': jax.random.normal(ks[2], (1,), dtype=jnp.float32) * 0.1, 'conv_w': jax.random.normal(ks[3], (C, 2 * C, 1, 1), dtype=jnp.float32) * (1.0 / np.sqrt(2 * C)), 'conv_b': jax.random.normal(ks[4], (C,), dtype=jnp.float32) * 0.1, 'convout_w': jax.random.normal(ks[5], (C, 2, 7, 7), dtype=jnp.float32) * (1.0 / np.sqrt(2 * 49)), 'convout_b': jax.random.normal(ks[6], (C,), dtype=jnp.float32) * 0.1}
    _L0_conv_all = _L0_conv_setup()
    _L0_conv_in = {k: v for k, v in _L0_conv_all.items() if k in ('mlp_w', 'mlp_b', 'conv_w', 'conv_b', 'convout_w', 'convout_b', )}
    del _L0_conv_all

    def _L1_conv_setup():
        import jax, jax.numpy as jnp
        import numpy as np

        def _directional_maxes(x):
            x1 = jax.lax.cummax(x, axis=2)
            x2 = jax.lax.cummax(x, axis=2, reverse=True)
            x_clk = jnp.rot90(x, k=-1, axes=(2, 3))
            x3 = jnp.rot90(jax.lax.cummax(x_clk, axis=2), k=1, axes=(2, 3))
            x4 = jnp.rot90(jax.lax.cummax(x_clk, axis=2, reverse=True), k=1, axes=(2, 3))
            return (x1, x2, x3, x4)
        key = jax.random.key(seed)
        k1, k2, k3 = jax.random.split(key, 3)
        B, C, H, W = (4, 32, 512, 512)
        x = jax.random.normal(k1, (B, C, H, W), dtype=jnp.float32)
        fan_in = 5 * C
        bound = 1.0 / np.sqrt(fan_in)
        Wc = jax.random.uniform(k2, (C, 5 * C, 1, 1), jnp.float32, -bound, bound)
        b = jax.random.uniform(k3, (C,), jnp.float32, -bound, bound)
        return {'x': x, 'W': Wc, 'b': b}
    _L1_conv_all = _L1_conv_setup()
    _L1_conv_in = {k: v for k, v in _L1_conv_all.items() if k in ('W', 'b', )}
    del _L1_conv_all

    return {
        "x": x,
        "L0_conv_mlp_w": _L0_conv_in["mlp_w"],
        "L0_conv_mlp_b": _L0_conv_in["mlp_b"],
        "L0_conv_conv_w": _L0_conv_in["conv_w"],
        "L0_conv_conv_b": _L0_conv_in["conv_b"],
        "L0_conv_convout_w": _L0_conv_in["convout_w"],
        "L0_conv_convout_b": _L0_conv_in["convout_b"],
        "L1_conv_W": _L1_conv_in["W"],
        "L1_conv_b": _L1_conv_in["b"],
    }

def reference(x, L0_conv_mlp_w, L0_conv_mlp_b, L0_conv_conv_w, L0_conv_conv_b, L0_conv_convout_w, L0_conv_convout_b, L1_conv_W, L1_conv_b):
    import jax
    import jax.numpy as jnp
    def _L0_conv_ref(x, mlp_w, mlp_b, conv_w, conv_b, convout_w, convout_b):
        import jax, jax.numpy as jnp
        import numpy as np
        from jax import lax
        PS = 2
        DN = ('NCHW', 'OIHW', 'NCHW')
        B, C, H, W = x.shape
        hn, wn = (H // PS, W // PS)
        xb = x.reshape(B, C, hn, PS, wn, PS)
        m = jnp.max(xb, axis=(3, 5))
        a = jnp.mean(xb, axis=(3, 5))
        gate = jax.nn.sigmoid((m + a) * mlp_w[0, 0] + 2.0 * mlp_b[0])
        product = (xb * gate[:, :, :, None, :, None]).reshape(B, C, H, W)
        cat = jnp.concatenate([product, x], axis=1)
        out = lax.conv_general_dilated(cat, conv_w, (1, 1), 'SAME', dimension_numbers=DN) + conv_b[None, :, None, None]
        fs = out
        cm = jnp.max(out, axis=1, keepdims=True)
        ca = jnp.mean(out, axis=1, keepdims=True)
        att = lax.conv_general_dilated(jnp.concatenate([cm, ca], axis=1), convout_w, (1, 1), 'SAME', dimension_numbers=DN)
        att = att + convout_b[None, :, None, None]
        return jax.nn.sigmoid(att) * fs

    def _L1_conv_ref(x, W, b):
        import jax, jax.numpy as jnp
        import numpy as np

        def _directional_maxes(x):
            x1 = jax.lax.cummax(x, axis=2)
            x2 = jax.lax.cummax(x, axis=2, reverse=True)
            x_clk = jnp.rot90(x, k=-1, axes=(2, 3))
            x3 = jnp.rot90(jax.lax.cummax(x_clk, axis=2), k=1, axes=(2, 3))
            x4 = jnp.rot90(jax.lax.cummax(x_clk, axis=2, reverse=True), k=1, axes=(2, 3))
            return (x1, x2, x3, x4)
        x1, x2, x3, x4 = _directional_maxes(x)
        x_con = jnp.concatenate((x, x1, x2, x3, x4), axis=1)
        out = jnp.einsum('bchw,oc->bohw', x_con, W[:, :, 0, 0])
        return out + b[None, :, None, None]

    def _gn(v, G=16, eps=1e-5):
        B_, C_, H_, W_ = v.shape
        g = v.reshape(B_, G, C_ // G, H_, W_)
        m = jnp.mean(g, axis=(2, 3, 4), keepdims=True)
        s = jnp.var(g, axis=(2, 3, 4), keepdims=True)
        return ((g - m) / jnp.sqrt(s + eps)).reshape(v.shape)

    def _ln_c(v, eps=1e-6):
        m = jnp.mean(v, axis=1, keepdims=True)
        s = jnp.var(v, axis=1, keepdims=True)
        return (v - m) / jnp.sqrt(s + eps)

    def _ln_t(v, eps=1e-5):
        m = jnp.mean(v, axis=-1, keepdims=True)
        s = jnp.var(v, axis=-1, keepdims=True)
        return (v - m) / jnp.sqrt(s + eps)

    def _to_tokens(v):
        B_, C_, H_, W_ = v.shape
        return v.reshape(B_, C_, H_ * W_).transpose(0, 2, 1)
    def _from_tokens(t, like):
        B_, C_, H_, W_ = like.shape
        return t.transpose(0, 2, 1).reshape(B_, C_, H_, W_)

    x = x + _L0_conv_ref(_gn(x), L0_conv_mlp_w, L0_conv_mlp_b, L0_conv_conv_w, L0_conv_conv_b, L0_conv_convout_w, L0_conv_convout_b)
    x = x + _L1_conv_ref(_gn(x), L1_conv_W, L1_conv_b)
    return x


_drawn_inputs = setup_inputs


def setup_inputs(seed=0):
    import zlib

    import numpy as np

    out = dict(_drawn_inputs(seed))
    spreads = {}
    factors = {'L0_conv_convout_b': 4.527}
    for name, (base, spread) in spreads.items():
        noise = np.random.default_rng([zlib.crc32(name.encode()), seed]).standard_normal(out[name].shape)
        drawn = base * np.exp(spread * noise) if base else spread * noise
        out[name] = jnp.asarray(drawn.astype(out[name].dtype))
    for name, factor in factors.items():
        out[name] = (out[name] * factor).astype(out[name].dtype)
    return out
```

```python
from contextlib import ExitStack

import numpy as np

import concourse.bass as bass
from concourse import mybir

F32 = mybir.dt.float32
BF16 = mybir.dt.bfloat16
ALU = mybir.AluOpType
ACT = mybir.ActivationFunctionType
AX_X = mybir.AxisListType.X

P = 128
LANES = 32
QUADS = P // LANES
STRIP = 16
UNROLL = 8
TAPS = 7
HALO = TAPS // 2
COLTAPS = 4
WIN = 8 + TAPS - 1
KCONV = COLTAPS * WIN * 2
SET = P // LANES
SUB = 2
GROUP = 2
EPS = 1e-5
LOWEST = -3.4028234663852886e38


def wait(eng, sem, value):
    if isinstance(value, int) and value <= 0:
        return
    eng.wait_ge(sem, value)


def passed(eng, sem):
    eng.sem_inc(sem, 1)


def build(nc, x, w_gated, w_plain, conv_b, w_att, att_b, mlp_w, mlp_b, w1, b1, same_group, eye, map_scale, y):
    B, C, H, W = x.shape
    NS = H // STRIP
    NJ = NS // UNROLL
    N = B * NS
    TILE = 4 * W
    PIECES = STRIP // SUB
    SETS = B // SET
    WB = W // LANES
    HW = H * W

    x1 = nc.dram_tensor("x1", [B, C, H, W], F32, kind="Internal").ap()
    maps = nc.dram_tensor("maps", [B, H + 2 * HALO, 2, W], F32, kind="Internal").ap()
    below = nc.dram_tensor("below", [B, C, NS + 1, QUADS, W], F32, kind="Internal").ap()

    def strip_of(t, img, strip, s):
        v = t.rearrange("b c (n g s r) w -> b n s c g (r w)", g=2, s=QUADS, r=2)
        return v[bass.ds(img, 1), bass.ds(strip, 1), s].rearrange("a b c g f -> (a b c) g f")

    def stage(img, j, u, lag):
        if u >= lag or not (isinstance(j, int) and j == 0):
            if isinstance(img, int) and img >= B:
                return None
            return img, UNROLL * j + u - lag, (img * NJ + j) * UNROLL + u - lag
        if isinstance(img, int) and img == 0:
            return None
        return img - 1, NS + u - lag, (img * NJ + j) * UNROLL + u - lag

    def uses(img, j, v, slots):
        return (img * NJ + j) * (UNROLL // slots) + v // slots

    def steps(eng, body, last=UNROLL):
        def bodies(img, j):
            for u in range(UNROLL):
                body(img, j, u)

        def rest(img):
            if NJ > 1:
                with eng.Fori(1, NJ) as j:
                    bodies(img, j)

        bodies(0, 0)
        rest(0)
        with eng.Fori(1, B) as img:
            bodies(img, 0)
            rest(img)
        for u in range(last):
            body(B, 0, u)

    with ExitStack() as ctx:
        def sb(name, shape, dt=F32, where=ctx):
            return where.enter_context(nc.sbuf_tensor(name, shape, dt))

        def sem(name):
            return ctx.enter_context(nc.semaphore(name))

        psum = [ctx.enter_context(nc.psum_tensor(f"bank{i}", [P, 512], F32)) for i in range(8)]

        passed_sp, passed_act, passed_dve = sem("passed_sp"), sem("passed_act"), sem("passed_dve")
        group_avg = sb("group_avg", [P, P])
        ident = sb("ident", [P, P])
        vecs = sb("vecs", [P, 8])
        conv_bias, att_bias, out_bias, mlpw, mlpb, mapscale = (vecs[:, i:i + 1] for i in range(6))
        xn_scale, xn_bias, gate_scale, gate_bias = (sb(n, [P, B]) for n in ("xn_scale", "xn_bias", "gate_scale", "gate_bias"))
        x1_sums = sb("x1_sums", [P, 2, N])

        with ExitStack() as a:
            xa = sb("xa", [P, UNROLL, TILE], where=a)
            zeros = sb("zeros", [P, 2 * W], where=a)
            lowest = sb("lowest", [P, QUADS * W], where=a)
            bn = sb("bn", [P, NS * 4, 6], where=a)
            mv = sb("mv", [P, 2], where=a)
            moments = sb("moments", [P, B, 2], where=a)
            avg = sb("avg", [P, B, 2], where=a)
            tmp = sb("tmp", [P, 4, B], where=a)

            consts_loaded = sem("consts_loaded")
            a_loaded = [sem(f"a_loaded{u}") for u in range(UNROLL)]
            a_strips = sem("a_strips")
            a_mv = sem("a_mv")
            a_mean = sem("a_mean")
            a_square = sem("a_square")
            a_moments = sem("a_moments")
            a_avg = sem("a_avg")
            a_chain = sem("a_chain")
            a_std = sem("a_std")
            fills = sem("fills")
            edges = sem("edges")

            with nc.Block() as block:
                @block.sync
                def _(sp):
                    sp.dma_start(group_avg[:, :], same_group).then_inc(consts_loaded, 16)
                    sp.dma_start(ident[:, :], eye).then_inc(consts_loaded, 16)
                    for i, v in enumerate((conv_b, att_b, b1, mlp_w, mlp_b, map_scale)):
                        sp.dma_start(vecs[:, i:i + 1], v).then_inc(consts_loaded, 16)

                    def body(img, j, u):
                        got = stage(img, j, u, 0)
                        if got is None:
                            return
                        at, t, n = got
                        wait(sp, a_strips, n - UNROLL + 1)
                        passed(sp, passed_sp)
                        for s in range(QUADS):
                            sp.dma_start(xa[LANES * s:LANES * (s + 1), u, :].rearrange("p (g f) -> p g f", g=2),
                                         strip_of(x, at, NS - 1 - t, s)).then_inc(a_loaded[u], 16)

                    steps(sp, body, 0)

                @block.gpsimd
                def _(pool):
                    pool.wait_ge(fills, 2)
                    for img in range(B):
                        for row in (0, H + HALO):
                            pool.dma_start(maps[img, row:row + HALO, :, :].rearrange("a m w -> a (m w)"),
                                           zeros[0:HALO, :]).then_inc(edges, 16)
                        pool.dma_start(below[img, :, NS].rearrange("c s w -> c (s w)"),
                                       lowest[0:C, :]).then_inc(edges, 16)
                    pool.wait_ge(edges, 16 * 3 * B)

                @block.tensor
                def _(pe):
                    pe.wait_ge(consts_loaded, 16 * 8)
                    pe.wait_ge(a_moments, B)
                    pe.matmul(psum[0][:, 0:2 * B], group_avg[:, :], moments[:, :, :].rearrange("p b k -> p (b k)"),
                              start=True, stop=True).then_inc(a_avg, 1)

                @block.scalar
                def _(act):
                    act.wait_ge(a_chain, 4)
                    act.activation(tmp[:, 1, :], tmp[:, 1, :], ACT.Sqrt).then_inc(a_std, 1)

                @block.vector
                def _(dve):
                    dve.memset(zeros[:, :], 0.0).then_inc(fills, 1)
                    dve.memset(lowest[:, :], LOWEST).then_inc(fills, 1)

                    def strips(img, j):
                        for u in range(UNROLL):
                            it = img * NJ + j
                            dve.wait_ge(a_loaded[u], (it + 1) * 16 * QUADS)
                            for k in range(4):
                                last = dve.bn_stats(bn[:, bass.ds((UNROLL * j + u) * 4 + k, 1), :].rearrange("p a k -> p (a k)"),
                                                    xa[:, u, k * W:(k + 1) * W])
                            last.then_inc(a_strips, 1)

                    with dve.Fori(0, B) as img:
                        with dve.Fori(0, NJ) as j:
                            strips(img, j)
                        dve.wait_ge(a_strips, (img + 1) * NS)
                        passed(dve, passed_dve)
                        dve.bn_aggr(mv[:, :], bn[:, :, :].rearrange("p a k -> p (a k)")).then_inc(a_mv, 1)
                        dve.wait_ge(a_mv, img + 1)
                        dve.tensor_copy(moments[:, bass.ds(img, 1), 0:1].rearrange("p a k -> p (a k)"), mv[:, 0:1]).then_inc(a_mean, 1)
                        dve.scalar_tensor_tensor(moments[:, bass.ds(img, 1), 1:2].rearrange("p a k -> p (a k)"), mv[:, 0:1], mv[:, 0:1],
                                                 mv[:, 1:2], ALU.mult, ALU.add).then_inc(a_moments, 1)
                        dve.wait_ge(a_moments, img + 1)
                        dve.wait_ge(a_mean, img + 1)
                    dve.wait_ge(a_avg, 1)
                    dve.tensor_copy(avg[:, :, :].rearrange("p b k -> p (b k)"), psum[0][:, 0:2 * B]).then_inc(a_chain, 1)
                    mean, square = avg[:, :, 0], avg[:, :, 1]
                    dve.wait_ge(a_chain, 1)
                    dve.tensor_tensor(tmp[:, 0, :], mean, mean, ALU.mult).then_inc(a_chain, 1)
                    dve.wait_ge(a_chain, 2)
                    dve.tensor_tensor(tmp[:, 1, :], square, tmp[:, 0, :], ALU.subtract).then_inc(a_chain, 1)
                    dve.wait_ge(a_chain, 3)
                    dve.tensor_scalar(tmp[:, 1, :], tmp[:, 1, :], 0.0, EPS, ALU.max, ALU.add).then_inc(a_chain, 1)
                    dve.wait_ge(a_std, 1)
                    dve.reciprocal(xn_scale[:, :], tmp[:, 1, :]).then_inc(a_chain, 1)
                    dve.wait_ge(a_chain, 5)
                    dve.scalar_tensor_tensor(xn_bias[:, :], mean, -1.0, xn_scale[:, :], ALU.mult, ALU.mult).then_inc(a_chain, 1)
                    dve.wait_ge(consts_loaded, 16 * 8)
                    dve.tensor_scalar(gate_scale[:, :], xn_scale[:, :], mlpw, None, ALU.mult).then_inc(a_chain, 1)
                    dve.wait_ge(a_chain, 7)
                    dve.tensor_scalar(tmp[:, 2, :], xn_bias[:, :], mlpw, 2.0, ALU.mult, ALU.mult).then_inc(a_chain, 1)
                    dve.tensor_scalar(tmp[:, 3, 0:1], mlpb, 2.0, None, ALU.mult).then_inc(a_chain, 1)
                    dve.wait_ge(a_chain, 9)
                    dve.tensor_scalar(gate_bias[:, :], tmp[:, 2, :], tmp[:, 3, 0:1], None, ALU.add).then_inc(a_chain, 1)
                    dve.wait_ge(a_chain, 10)

        with ExitStack() as b:
            wg = sb("wg", [P, P], where=b)
            wp = sb("wp", [P, P], where=b)
            wa = sb("wa", [KCONV, 2, 2, P], where=b)
            xs = sb("xs", [P, UNROLL, TILE], where=b)
            xn = sb("xn", [P, 2, TILE], where=b)
            gated = sb("gated", [P, 2, TILE], where=b)
            fs = sb("fs", [P, 4, TILE], where=b)
            att = sb("att", [P, 2, TILE], where=b)
            win = sb("win", [KCONV, 2, 2, W + 4], where=b)
            pair_max = sb("pair_max", [P, 2, W], where=b)
            below_pair = sb("below_pair", [P, 2, W], where=b)
            pool_max = sb("pool_max", [P, 2, W // 2], where=b)
            gate_in = sb("gate_in", [P, 2, 2, W // 2], where=b)
            pair_sum = sb("pair_sum", [P, 2, W], where=b)
            pool_sum = sb("pool_sum", [P, 2, 2, W // 2], where=b)
            gate = sb("gate", [P, 2, 2, W // 2], where=b)
            run_max = sb("run_max", [P, 2, W], where=b)
            map_cols = sb("map_cols", [P, 2, P], where=b)
            map_rows = sb("map_rows", [P, 2, P], where=b)
            unused = sb("unused", [P, TILE], BF16, where=b)

            names = ("weights_loaded wg_edges x_pair_sums pool_sums pair_maxes pool_maxes gate_ins xns gates gateds "
                     "out_rows fs_rows reduced transposed map_rows_ready att_rows sig_rows products x1s "
                     "below_pairs below_rows below_ready sums_taken win_cleared").split()
            s_ = {k: sem(k) for k in names}
            x_loaded = [sem(f"x_loaded{u}") for u in range(UNROLL)]
            x1_stored = [sem(f"x1_stored{u}") for u in range(UNROLL)]
            maps_stored = [sem(f"maps_stored{u}") for u in range(2)]
            below_stored = [sem(f"below_stored{u}") for u in range(2)]
            win_loaded = [sem(f"win_loaded{u}") for u in range(2)]
            (weights_loaded, _, x_pair_sums, pool_sums, pair_maxes, pool_maxes, gate_ins, xns, gates, gateds,
             out_rows, fs_rows, reduced, transposed, map_rows_ready, att_rows, sig_rows, products, x1s,
             below_pairs, below_rows, below_ready, sums_taken, win_cleared) = (s_[k] for k in names)

            def grw(tile):
                return tile.rearrange("p (g r w) -> p g r w", g=2, r=2)

            att_bank = (4, 5, 6, 4)
            att_bank_read = (0, -2, -1, 1)
            ROWS = 4

            with nc.Block() as block:
                @block.sync
                def _(sp):
                    sp.dma_start(wg[:, :], w_gated).then_inc(weights_loaded, 16)
                    sp.dma_start(wp[:, :], w_plain).then_inc(weights_loaded, 16)
                    sp.dma_start(wa[:, :, :, :], w_att).then_inc(weights_loaded, 16)

                    def body(img, j, u):
                        if got := stage(img, j, u, 4):
                            at, t, n = got
                            wait(sp, map_rows_ready, n + 1)
                            passed(sp, passed_sp)
                            k = n_slot(u, 4)
                            for g in range(2):
                                row = HALO + STRIP * (NS - 1 - t) + 8 * g
                                rows = maps[bass.ds(at, 1), bass.ds(row, 8)].rearrange(
                                    "a (s r) m (k w) -> (a r m k) s w", s=QUADS, w=LANES)
                                sp.dma_start(rows, map_rows[64 * g:64 * (g + 1), k, :].rearrange(
                                    "p (s w) -> p s w", s=QUADS)).then_inc(maps_stored[k], 16)
                        if got := stage(img, j, u, 5):
                            at, t, n = got
                            if isinstance(n, int) and n == N - 1:
                                sp.wait_ge(maps_stored[n % 2], 32 * (N // 2))
                            else:
                                sp.wait_ge(maps_stored[n_slot(u, 4)], 32 * (uses(img, j, u - 4, 2) + 1))
                            passed(sp, passed_sp)
                            wait(sp, att_rows, ROWS * (n - 1))
                            passed(sp, passed_sp)
                            for k in range(COLTAPS):
                                row = STRIP * (NS - 1 - t)
                                for g in range(2):
                                    sp.dma_start(
                                        win[2 * WIN * k:2 * WIN * (k + 1), n_slot(u, 5), g, HALO - k:HALO - k + W],
                                        maps[bass.ds(at, 1), bass.ds(row + 8 * g, WIN)].rearrange("a r m w -> (a r m) w")
                                    ).then_inc(win_loaded[n_slot(u, 5)], 16)
                        if got := stage(img, j, u, 0):
                            at, t, n = got
                            it = img * NJ + j
                            wait(sp, x1_stored[u], 16 * QUADS * it)
                            passed(sp, passed_sp)
                            wait(sp, sums_taken, 2 * (n - UNROLL + 1))
                            wait(sp, below_pairs, n - UNROLL + 1)
                            passed(sp, passed_sp)
                            for s in range(QUADS):
                                sp.dma_start(xs[LANES * s:LANES * (s + 1), u, :].rearrange("p (g f) -> p g f", g=2),
                                             strip_of(x, at, NS - 1 - t, s)).then_inc(x_loaded[u], 16)
                        if got := stage(img, j, u, 7):
                            at, t, n = got
                            wait(sp, x1s, n + 1)
                            passed(sp, passed_sp)
                            v = (u - 7) % UNROLL
                            for s in range(QUADS):
                                sp.dma_start(strip_of(x1, at, NS - 1 - t, s),
                                             xs[LANES * s:LANES * (s + 1), v, :].rearrange("p (g f) -> p g f", g=2)
                                             ).then_inc(x1_stored[v], 16)
                        if got := stage(img, j, u, 8):
                            at, t, n = got
                            wait(sp, below_ready, n + 1)
                            passed(sp, passed_sp)
                            dst = below[bass.ds(at, 1), :, bass.ds(NS - 1 - t, 1)].rearrange("a c n s w -> s (a c n) w")
                            sp.dma_start(dst, run_max[:, n_slot(u, 8), :]).then_inc(below_stored[n_slot(u, 8)], 16)

                    def n_slot(u, lag, slots=2):
                        return (u - lag) % slots

                    steps(sp, body)
                    for v in range(UNROLL):
                        sp.wait_ge(x1_stored[v], 16 * QUADS * (N // UNROLL))
                    for k in range(2):
                        sp.wait_ge(below_stored[k], 16 * (N // 2))
                        sp.wait_ge(maps_stored[k], 32 * (N // 2))

                @block.gpsimd
                def _(pool):
                    def body(img, j, u):
                        if got := stage(img, j, u, 1):
                            _, _, n = got
                            k = (u - 1) % 2
                            pool.wait_ge(gates, n + 1)
                            pool.wait_ge(xns, n + 1)
                            wait(pool, out_rows, ROWS * (n - 1))
                            for g in range(2):
                                src = grw(xn[:, k, :])[:, g].rearrange("p r (w d) -> p r w d", d=2)
                                dst = grw(gated[:, k, :])[:, g].rearrange("p r (w d) -> p r w d", d=2)
                                by = gate[:, k, g, :].unsqueeze(1).unsqueeze(3).broadcast_to([P, 2, W // 2, 2])
                                last = pool.tensor_tensor(dst, src, by, ALU.mult)
                            last.then_inc(gateds, 1)
                        if got := stage(img, j, u, 0):
                            _, _, n = got
                            it = img * NJ + j
                            rows = grw(xs[:, u, :])
                            pool.wait_ge(x_loaded[u], 16 * QUADS * (it + 1))
                            wait(pool, pool_sums, n)
                            pool.tensor_tensor(pair_sum[:, :, :], rows[:, :, 0], rows[:, :, 1], ALU.add).then_inc(x_pair_sums, 1)
                            pool.wait_ge(x_pair_sums, n + 1)
                            wait(pool, gate_ins, n - 1)
                            pairs = pair_sum[:, :, :].rearrange("p g (w d) -> p g w d", d=2)
                            pool.tensor_tensor(pool_sum[:, u % 2], pairs[:, :, :, 0], pairs[:, :, :, 1], ALU.add).then_inc(pool_sums, 1)
                        if got := stage(img, j, u, 6):
                            _, _, n = got
                            v = (u - 6) % UNROLL
                            pool.wait_ge(products, n + 1)
                            pool.tensor_tensor(xs[:, v, :], xs[:, v, :], att[:, (u - 6) % 2, :], ALU.add).then_inc(x1s, 1)

                    steps(pool, body)

                @block.scalar
                def _(act):
                    def body(img, j, u):
                        if got := stage(img, j, u, 1):
                            at, _, n = got
                            k = (u - 1) % 2
                            act.wait_ge(gate_ins, n + 1)
                            wait(act, gateds, n - 1)
                            passed(act, passed_act)
                            act.activation(gate[:, k], gate_in[:, k], ACT.Sigmoid,
                                           scale=gate_scale[:, bass.ds(at, 1)], bias=gate_bias[:, bass.ds(at, 1)]).then_inc(gates, 1)
                        if got := stage(img, j, u, 1):
                            at, _, n = got
                            it = uses(img, j, u - 1, UNROLL)
                            act.wait_ge(x_loaded[(u - 1) % UNROLL], 16 * QUADS * (it + 1))
                            wait(act, out_rows, ROWS * (n - 1))
                            passed(act, passed_act)
                            act.activation(xn[:, (u - 1) % 2, :], xs[:, (u - 1) % UNROLL, :], ACT.Identity, scale=xn_scale[:, bass.ds(at, 1)],
                                           bias=xn_bias[:, bass.ds(at, 1)]).then_inc(xns, 1)
                        if got := stage(img, j, u, 2):
                            _, _, n = got
                            wait(act, products, n - 3)
                            for q in range(ROWS):
                                act.wait_ge(out_rows, ROWS * n + q + 1)
                                act.activation(fs[:, (u - 2) % 4, q * W:(q + 1) * W], psum[q][:, 0:W], ACT.Identity,
                                               bias=conv_bias).then_inc(fs_rows, 1)
                        if got := stage(img, j, u, 3):
                            _, _, n = got
                            act.wait_ge(transposed, n + 1)
                            wait(act, maps_stored[(u - 3) % 2], 32 * uses(img, j, u - 3, 2))
                            act.activation(map_rows[:, (u - 3) % 2, :], psum[7][:, 0:P], ACT.Identity,
                                           scale=mapscale).then_inc(map_rows_ready, 1)
                        if got := stage(img, j, u, 7):
                            _, _, n = got
                            v = (u - 7) % UNROLL
                            act.wait_ge(x1s, n + 1)
                            for k, f in enumerate((ACT.Identity, ACT.Square)):
                                wait(act, sums_taken, 2 * n + k)
                                passed(act, passed_act)
                                act.activation(unused[:, :], xs[:, v, :], f,
                                               accum_out=x1_sums[:, k, bass.ds(n, 1)]).then_inc(sums_taken, 1)
                        if got := stage(img, j, u, 5):
                            _, _, n = got
                            wait(act, x1s, n - 1)
                            for q in range(ROWS):
                                act.wait_ge(att_rows, ROWS * n + q + 1)
                                act.activation(att[:, (u - 5) % 2, q * W:(q + 1) * W], psum[att_bank[q]][:, 0:W],
                                               ACT.Sigmoid, bias=att_bias).then_inc(sig_rows, 1)

                    steps(act, body)

                @block.vector
                def _(dve):
                    dve.memset(win[:, :, :, :], 0.0).then_inc(win_cleared, 1)

                    def body(img, j, u):
                        maps_now, out_now = stage(img, j, u, 3), stage(img, j, u, 6)
                        pool_now, below_now = stage(img, j, u, 0), stage(img, j, u, 7)
                        if maps_now:
                            _, _, o = maps_now
                            dve.wait_ge(fs_rows, ROWS * (o + 1))
                            wait(dve, transposed, o - 1)
                            cols = map_cols[:, (u - 3) % 2, :].rearrange("p (q m k) -> p q m k", m=2, k=WB)
                            src = fs[:, (u - 3) % 4, :].rearrange("p (q k c) -> p q k c", q=ROWS, c=LANES)
                            for m, op in enumerate((ALU.max, ALU.add)):
                                dve.tensor_reduce(cols[:, :, m, :], src, AX_X, op, apply_transpose=True).then_inc(reduced, 1)
                        if out_now:
                            _, _, p = out_now
                            dve.wait_ge(sig_rows, ROWS * (p + 1))
                            dve.tensor_tensor(att[:, (u - 6) % 2, :], att[:, (u - 6) % 2, :], fs[:, (u - 6) % 4, :],
                                              ALU.mult).then_inc(products, 1)
                        if pool_now:
                            _, _, n = pool_now
                            rows = grw(xs[:, u, :])
                            dve.wait_ge(x_loaded[u], 16 * QUADS * (uses(img, j, u, UNROLL) + 1))
                            dve.tensor_tensor(pair_max[:, :, :], rows[:, :, 0], rows[:, :, 1], ALU.max).then_inc(pair_maxes, 1)
                        if below_now:
                            _, t_below, b = below_now
                            k = (u - 7) % 2
                            rows = grw(xs[:, (u - 7) % UNROLL, :])
                            first = isinstance(t_below, int) and t_below == 0
                            dve.wait_ge(x1s, b + 1)
                            wait(dve, below_ready, b)
                            dve.tensor_tensor(below_pair[:, :, :], rows[:, :, 0], rows[:, :, 1], ALU.max).then_inc(below_pairs, 1)
                        if pool_now:
                            dve.wait_ge(pair_maxes, n + 1)
                            wait(dve, gate_ins, n)
                            pairs = pair_max[:, :, :].rearrange("p g (w d) -> p g w d", d=2)
                            dve.tensor_tensor(pool_max[:, :, :], pairs[:, :, :, 0], pairs[:, :, :, 1], ALU.max).then_inc(pool_maxes, 1)
                        if below_now:
                            dve.wait_ge(below_pairs, b + 1)
                            wait(dve, below_stored[k], 16 * uses(img, j, u - 7, 2))
                            dve.tensor_tensor(run_max[:, k, :], below_pair[:, 0, :], below_pair[:, 1, :],
                                              ALU.max).then_inc(below_rows, 1)
                        if pool_now:
                            dve.wait_ge(pool_maxes, n + 1)
                            dve.wait_ge(pool_sums, n + 1)
                            wait(dve, gates, n - 1)
                            dve.scalar_tensor_tensor(gate_in[:, u % 2], pool_sum[:, u % 2], 0.25, pool_max[:, :, :],
                                                     ALU.mult, ALU.add).then_inc(gate_ins, 1)
                        if below_now:
                            dve.wait_ge(below_rows, b + 1)
                            wait(dve, below_ready, b)
                            if first:
                                dve.tensor_scalar(run_max[:, k, :], run_max[:, k, :], LOWEST, None, ALU.max).then_inc(below_ready, 1)
                            else:
                                dve.tensor_tensor(run_max[:, k, :], run_max[:, k, :], run_max[:, 1 - k, :],
                                                  ALU.max).then_inc(below_ready, 1)

                    steps(dve, body)

                @block.tensor
                def _(pe):
                    pe.wait_ge(weights_loaded, 48)

                    def body(img, j, u):
                        if got := stage(img, j, u, 0):
                            _, _, n = got
                            pe.wait_ge(xns, n + 1)
                            for q in range(ROWS):
                                wait(pe, fs_rows, ROWS * (n - 1) + q + 1)
                                pe.matmul(psum[q][:, 0:W], wp[:, :], xn[:, u % 2, q * W:(q + 1) * W], start=True, stop=False)
                            pe.wait_ge(gateds, n + 1)
                            for q in range(ROWS):
                                pe.matmul(psum[q][:, 0:W], wg[:, :], gated[:, u % 2, q * W:(q + 1) * W],
                                          start=False, stop=True).then_inc(out_rows, 1)
                        if got := stage(img, j, u, 1):
                            _, _, n = got
                            pe.wait_ge(reduced, 2 * (n + 1))
                            wait(pe, map_rows_ready, n)
                            pe.transpose(psum[7][:, 0:P], map_cols[:, (u - 1) % 2, :], ident[:, :]).then_inc(transposed, 1)
                        if got := stage(img, j, u, 3):
                            _, _, n = got
                            k = (u - 3) % 2
                            pe.wait_ge(win_loaded[k], 16 * 2 * COLTAPS * (uses(img, j, u - 3, 2) + 1))
                            for q in range(ROWS):
                                g, r = divmod(q, 2)
                                wait(pe, sig_rows, ROWS * n + att_bank_read[q])
                                for half in range(2):
                                    last = pe.matmul(psum[att_bank[q]][:, 0:W], wa[:, r, half, :],
                                                     win[:, k, g, COLTAPS * half:COLTAPS * half + W],
                                                     start=(half == 0), stop=(half == 1))
                                last.then_inc(att_rows, 1)

                    steps(pe, body)

        with ExitStack() as c:
            w_raw = sb("w_raw", [P, 5, P], where=c)
            w_now = sb("w_now", [P, 5, P], where=c)
            spread = sb("spread", [P, 2, P], where=c)
            share = sb("share", [P, 1], where=c)
            sums = sb("sums", [P, 2, B], where=c)
            st = sb("st", [P, 8], where=c)
            xt = sb("xt", [P, 2, STRIP, W], where=c)
            up = sb("up", [P, 2, STRIP, W], where=c)
            down = sb("down", [P, 2 * SUB, W], where=c)
            right = sb("right", [P, 2 * SUB, W], where=c)
            left = sb("left", [P, 2 * SUB, W], where=c)
            bl = sb("bl", [P, QUADS, W], where=c)
            yt = sb("yt", [P, 2, 2 * SUB, W], where=c)

            names = ("c_weights summed spread_ready set_moments c_chain c_std c_scaled bias_mm set_ready bl_loaded bl_max "
                     "up_rows down_rows right_rows left_rows y_rows y_out y_stored0 y_stored1 top_cleared").split()
            s_ = {k: sem(k) for k in names}
            (c_weights, summed, spread_ready, set_moments, c_chain, c_std, c_scaled, bias_mm, set_ready, bl_loaded, bl_max,
             up_rows, down_rows, right_rows, left_rows, y_rows, y_out, y_stored0, y_stored1, top_cleared) = (s_[k] for k in names)
            y_stored = (y_stored0, y_stored1)
            x1_loaded = [[sem(f"c_loaded{k}_{p}") for p in range(4)] for k in range(2)]
            QROWS = STRIP // 4
            RING = 2 * SUB
            YROWS = 2 * SUB
            NT = SETS * NS

            x1_v = x1.rearrange("b c h w -> (b c) h w")
            y_v = y.rearrange("b c h w -> (b c) h w")
            below_v = below.rearrange("b c n s w -> (b c) n s w")

            with nc.Block() as block:
                @block.sync
                def _(sp):
                    sp.dma_start(w_raw[:, :, :], w1).then_inc(c_weights, 16)

                    def load(g, i, k):
                        tile, n = 2 * i + k, NS * g + 2 * i + k
                        wait(sp, up_rows, STRIP * (n - 1) + 1)
                        passed(sp, passed_sp)
                        sp.dma_start(bl[:, :, :], below_v[bass.ds(P * g, P), bass.ds(tile + 1, 1)].rearrange(
                            "p n s w -> p (n s) w")).then_inc(bl_loaded, 16)
                        for q in range(4):
                            wait(sp, y_rows, STRIP * (n - 2) + QROWS * (q + 1))
                            passed(sp, passed_sp)
                            sp.dma_start(xt[:, k, QROWS * q:QROWS * (q + 1), :],
                                         x1_v[bass.ds(P * g, P), bass.ds(STRIP * tile + QROWS * q, QROWS)]
                                         ).then_inc(x1_loaded[k][q], 16)

                    for k in range(2):
                        load(0, 0, k)
                    if NS > 2:
                        with sp.Fori(1, NS // 2) as i:
                            for k in range(2):
                                load(0, i, k)
                    with sp.Fori(1, SETS) as g:
                        with sp.Fori(0, NS // 2) as i:
                            for k in range(2):
                                load(g, i, k)

                @block.gpsimd
                def _(pool):
                    def store(g, i):
                        for k in range(2):
                            tile, n = 2 * i + k, NS * g + 2 * i + k
                            for p in range(STRIP // YROWS):
                                pool.wait_ge(y_out, STRIP * n + YROWS * (p + 1))
                                pool.dma_start(y_v[bass.ds(P * g, P), bass.ds(STRIP * tile + YROWS * p, YROWS)],
                                               yt[:, p % 2]).then_inc(y_stored[p % 2], 16)

                    with pool.Fori(0, SETS) as g:
                        with pool.Fori(0, NS // 2) as i:
                            store(g, i)
                    for v in range(2):
                        pool.wait_ge(y_stored[v], 16 * NT * (STRIP // YROWS // 2))

                @block.scalar
                def _(act):
                    def emit(g, i):
                        for k in range(2):
                            n = NS * g + 2 * i + k
                            for h in range(STRIP):
                                p = h // YROWS
                                if h % YROWS == 0:
                                    wait(act, y_stored[p % 2], 16 * (2 * n + p // 2))
                                act.wait_ge(y_rows, STRIP * n + h + 1)
                                act.activation(yt[:, p % 2, h % YROWS, :], psum[h % 4][:, 0:W], ACT.Identity,
                                               bias=st[:, 6:7]).then_inc(y_out, 1)

                    def prepare(g):
                        act.wait_ge(c_chain, 5 * g + 4)
                        act.activation(st[:, 2:3], st[:, 2:3], ACT.Sqrt).then_inc(c_std, 1)
                        act.wait_ge(set_ready, 2 * (g + 1))

                    prepare(0)
                    emit(0, 0)
                    if NS > 2:
                        with act.Fori(1, NS // 2) as i:
                            emit(0, i)
                    with act.Fori(1, SETS) as g:
                        prepare(g)
                        with act.Fori(0, NS // 2) as i:
                            emit(g, i)

                @block.tensor
                def _(pe):
                    def prepare(g):
                        pe.wait_ge(spread_ready, 8 * (g + 1))
                        for k in range(2):
                            last = pe.matmul(psum[4][:, k:k + 1], spread[:, k, :], share[:, :], start=True, stop=True)
                        last.then_inc(set_moments, 1)
                        pe.wait_ge(c_scaled, 5 * (g + 1))
                        for k in range(5):
                            last = pe.matmul(psum[5][:, 0:1], w_now[:, k, :], st[:, 5:6], start=(k == 0), stop=(k == 4))
                        last.then_inc(bias_mm, 1)
                        pe.wait_ge(set_ready, 2 * (g + 1))

                    def multiply(g, i):
                        for k in range(2):
                            n = NS * g + 2 * i + k
                            for h in range(STRIP):
                                row = STRIP * n + h
                                bank = psum[h % 4][:, 0:W]
                                wait(pe, y_out, row - 3)
                                if h % QROWS == 0:
                                    pe.wait_ge(x1_loaded[k][h // QROWS], 16 * ((NS // 2) * g + i + 1))
                                if h == 0:
                                    pe.wait_ge(up_rows, STRIP * (n + 1))
                                pe.matmul(bank, w_now[:, 0, :], xt[:, k, h, :], start=True, stop=False)
                                pe.matmul(bank, w_now[:, 2, :], up[:, k, h, :], start=False, stop=False)
                                pe.wait_ge(down_rows, row + 1)
                                pe.matmul(bank, w_now[:, 1, :], down[:, h % RING, :], start=False, stop=False)
                                pe.wait_ge(right_rows, row + 1)
                                pe.matmul(bank, w_now[:, 3, :], right[:, h % RING, :], start=False, stop=False)
                                pe.wait_ge(left_rows, row + 1)
                                pe.matmul(bank, w_now[:, 4, :], left[:, h % RING, :], start=False, stop=True).then_inc(y_rows, 1)

                    prepare(0)
                    multiply(0, 0)
                    if NS > 2:
                        with pe.Fori(1, NS // 2) as i:
                            multiply(0, i)
                    with pe.Fori(1, SETS) as g:
                        prepare(g)
                        with pe.Fori(0, NS // 2) as i:
                            multiply(g, i)

                @block.vector
                def _(dve):
                    dve.memset(share[:, :], QUADS * GROUP / (GROUP * HW)).then_inc(summed, 1)
                    for k in range(2):
                        dve.tensor_reduce(sums[:, k, :], x1_sums[:, k, :].rearrange("p (b n) -> p b n", n=NS), AX_X,
                                          ALU.add).then_inc(summed, 1)
                    dve.wait_ge(summed, 3)
                    dve.wait_ge(c_weights, 16)

                    def prepare(g):
                        wait(dve, y_rows, STRIP * NS * g)
                        wait(dve, y_out, STRIP * NS * g)
                        for k in range(2):
                            for a in range(SET):
                                dve.tensor_scalar(spread[:, k, LANES * a:LANES * (a + 1)], group_avg[:, 0:LANES],
                                                  sums[:, k, bass.ds(SET * g + a, 1)], None, ALU.mult).then_inc(spread_ready, 1)
                        dve.wait_ge(set_moments, g + 1)
                        dve.tensor_copy(st[:, 0:2], psum[4][:, 0:2]).then_inc(c_chain, 1)
                        dve.wait_ge(c_chain, 5 * g + 1)
                        dve.tensor_scalar(st[:, 5:6], st[:, 0:1], -1.0, None, ALU.mult).then_inc(c_chain, 1)
                        dve.wait_ge(c_chain, 5 * g + 2)
                        dve.scalar_tensor_tensor(st[:, 2:3], st[:, 0:1], st[:, 5:6], st[:, 1:2], ALU.mult, ALU.add).then_inc(c_chain, 1)
                        dve.wait_ge(c_chain, 5 * g + 3)
                        dve.tensor_scalar(st[:, 2:3], st[:, 2:3], 0.0, EPS, ALU.max, ALU.add).then_inc(c_chain, 1)
                        dve.wait_ge(c_std, g + 1)
                        dve.reciprocal(st[:, 3:4], st[:, 2:3]).then_inc(c_chain, 1)
                        dve.wait_ge(c_chain, 5 * g + 5)
                        for k in range(5):
                            dve.tensor_scalar(w_now[:, k, :], w_raw[:, k, :], st[:, 3:4], None, ALU.mult).then_inc(c_scaled, 1)
                        dve.wait_ge(bias_mm, g + 1)
                        dve.tensor_tensor(st[:, 6:7], psum[5][:, 0:1], out_bias, ALU.add).then_inc(set_ready, 1)
                        dve.tensor_tensor(w_now[:, 0, :], w_now[:, 0, :], ident[:, :], ALU.add).then_inc(set_ready, 1)
                        dve.memset(down[:, RING - 1, :], LOWEST).then_inc(top_cleared, 1)
                        dve.wait_ge(top_cleared, g + 1)

                    def up_start(n):
                        dve.wait_ge(bl_loaded, 16 * (n + 1))
                        dve.tensor_tensor(bl[:, 0, :], bl[:, 0, :], bl[:, 1, :], ALU.max).then_inc(bl_max, 1)
                        dve.tensor_tensor(bl[:, 2, :], bl[:, 2, :], bl[:, 3, :], ALU.max).then_inc(bl_max, 1)
                        dve.wait_ge(bl_max, 3 * n + 2)
                        dve.tensor_tensor(bl[:, 0, :], bl[:, 0, :], bl[:, 2, :], ALU.max).then_inc(bl_max, 1)

                    def up_row(g, i, k, n, h):
                        if h % QROWS == QROWS - 1:
                            dve.wait_ge(x1_loaded[k][h // QROWS], 16 * ((NS // 2) * g + i + 1))
                        if h == STRIP - 1:
                            dve.wait_ge(bl_max, 3 * n + 3)
                            dve.tensor_tensor(up[:, k, h, :], xt[:, k, h, :], bl[:, 0, :], ALU.max).then_inc(up_rows, 1)
                        else:
                            dve.wait_ge(up_rows, STRIP * n + STRIP - 1 - h)
                            dve.tensor_tensor(up[:, k, h, :], xt[:, k, h, :], up[:, k, h + 1, :], ALU.max).then_inc(up_rows, 1)

                    def row(k, n, h):
                        at = STRIP * n + h
                        ring = h % RING
                        src = xt[:, k, h, :]
                        wait(dve, y_rows, at - RING + 1)
                        if isinstance(at, int) and at == 0:
                            pass
                        else:
                            dve.wait_ge(down_rows, at)
                        dve.tensor_tensor(down[:, ring, :], src, down[:, (ring - 1) % RING, :], ALU.max).then_inc(down_rows, 1)
                        dve.tensor_tensor_scan(right[:, ring, :], src, src, LOWEST, ALU.max, ALU.max).then_inc(right_rows, 1)
                        dve.tensor_tensor_scan(left[:, ring, ::-1], src[:, ::-1], src[:, ::-1], LOWEST, ALU.max, ALU.max).then_inc(left_rows, 1)

                    def tile(g, i, k, following):
                        n = NS * g + 2 * i + k
                        for h in range(STRIP):
                            row(k, n, h)
                            if following and h >= STRIP // 2:
                                fg, fi, fk = following
                                if h == STRIP // 2:
                                    up_start(n + 1)
                                for e in range(2):
                                    up_row(fg, fi, fk, n + 1, STRIP - 1 - 2 * (h - STRIP // 2) - e)

                    def whole(g):
                        prepare(g)
                        up_start(NS * g)
                        for h in range(STRIP - 1, -1, -1):
                            up_row(g, 0, 0, NS * g, h)

                    whole(0)
                    tile(0, 0, 0, (0, 0, 1))
                    if NS > 2:
                        tile(0, 0, 1, (0, 1, 0))
                        if NS > 4:
                            with dve.Fori(1, NS // 2 - 1) as i:
                                tile(0, i, 0, (0, i, 1))
                                tile(0, i, 1, (0, i + 1, 0))
                        tile(0, NS // 2 - 1, 0, (0, NS // 2 - 1, 1))
                    tile(0, NS // 2 - 1, 1, None)
                    with dve.Fori(1, SETS) as g:
                        whole(g)
                        if NS > 2:
                            with dve.Fori(0, NS // 2 - 1) as i:
                                tile(g, i, 0, (g, i, 1))
                                tile(g, i, 1, (g, i + 1, 0))
                        tile(g, NS // 2 - 1, 0, (g, NS // 2 - 1, 1))
                        tile(g, NS // 2 - 1, 1, None)


def blocks(w):
    out = np.zeros((QUADS, LANES, QUADS, LANES), w.dtype)
    for s in range(QUADS):
        out[s, :, s, :] = w.T
    return out.reshape(P, P)


def attention_blocks(w):
    out = np.zeros((COLTAPS, WIN, 2, 2, 2, QUADS, LANES), w.dtype)
    for half in range(2):
        for k in range(COLTAPS):
            j = COLTAPS * half + k
            if j < TAPS:
                for r in range(2):
                    for s in range(QUADS):
                        for i in range(TAPS):
                            out[k, 2 * s + r + i, :, r, half, s, :] = w[:, :, i, j].T
    return out.reshape(KCONV, 2, 2, P)


def layout(v):
    C = v["x"].shape[1]
    tile = lambda a: np.ascontiguousarray(np.tile(np.asarray(a).reshape(-1), P // np.asarray(a).size).reshape(P, 1))
    lane = np.arange(P) % LANES // GROUP
    same = (lane[:, None] == lane[None, :]).astype(np.float32) / (QUADS * GROUP)
    scale = np.where(np.arange(P) // (P // 8) % 2 == 0, 1.0, 1.0 / LANES).astype(np.float32).reshape(P, 1)
    conv_w = v["L0_conv_conv_w"][:, :, 0, 0]
    out_w = v["L1_conv_W"][:, :, 0, 0]
    return {
        "x": np.ascontiguousarray(v["x"]),
        "w_gated": blocks(conv_w[:, :C]),
        "w_plain": blocks(conv_w[:, C:]),
        "conv_b": tile(v["L0_conv_conv_b"]),
        "w_att": attention_blocks(v["L0_conv_convout_w"]),
        "att_b": tile(v["L0_conv_convout_b"]),
        "mlp_w": tile(v["L0_conv_mlp_w"]),
        "mlp_b": tile(v["L0_conv_mlp_b"]),
        "w1": np.ascontiguousarray(np.stack([blocks(out_w[:, C * k:C * (k + 1)]) for k in range(5)], axis=1)),
        "b1": tile(v["L1_conv_b"]),
        "same_group": same,
        "eye": np.eye(P, dtype=np.float32),
        "map_scale": scale,
    }


def kernel(**inputs):
    import concourse.bacc as bacc
    from concourse.bass_utils import run_bass_kernel_spmd

    arrays = layout({k: np.asarray(a) for k, a in inputs.items()})
    nc = bacc.Bacc("TRN2", target_bir_lowering=False, num_devices=1)
    args = {k: nc.dram_tensor(f"in_{k}", a.shape, mybir.dt.from_np(a.dtype), kind="ExternalInput").ap()
            for k, a in arrays.items()}
    y = nc.dram_tensor("out_y", arrays["x"].shape, F32, kind="ExternalOutput").ap()
    build(nc, y=y, **args)
    result = run_bass_kernel_spmd(nc, [{f"in_{k}": a for k, a in arrays.items()}], core_ids=[0])
    return result.results[0]["out_y"]
```

```python
from contextlib import ExitStack

import numpy as np

import concourse.bass as bass
from concourse import mybir

F32 = mybir.dt.float32
BF16 = mybir.dt.bfloat16
F32R = mybir.dt.float32r
ALU = mybir.AluOpType
ACT = mybir.ActivationFunctionType
AX_X = mybir.AxisListType.X

P = 128
LANES = 32
QUADS = P // LANES
STRIP = 16
UNROLL = 8
TAPS = 7
HALO = TAPS // 2
COLTAPS = 4
WIN = 8 + TAPS - 1
KCONV = COLTAPS * WIN * 2
SET = P // LANES
SUB = 2
GROUP = 2
EPS = 1e-5
LOWEST = -3.4028234663852886e38


def wait(eng, sem, value):
    if isinstance(value, int) and value <= 0:
        return
    eng.wait_ge(sem, value)


def passed(eng, sem):
    eng.sem_inc(sem, 1)


def build(nc, x, w_gated, w_plain, conv_b, w_att, att_b, mlp_w, mlp_b, w1, b1, same_group, eye, map_scale, y):
    B, C, H, W = x.shape
    NS = H // STRIP
    NJ = NS // UNROLL
    N = B * NS
    TILE = 4 * W
    PIECES = STRIP // SUB
    SETS = B // SET
    WB = W // LANES
    HW = H * W

    x1 = nc.dram_tensor("x1", [B, C, H, W], F32, kind="Internal").ap()
    maps = nc.dram_tensor("maps", [2, B, H + 2 * HALO, 2, W], F32, kind="Internal").ap()
    below = nc.dram_tensor("below", [B, C, NS + 1, QUADS, W], F32, kind="Internal").ap()

    def strip_of(t, img, strip, g):
        v = t.rearrange("b c (n g s r) w -> b n g s c (r w)", g=2, s=QUADS, r=2)
        return v[bass.ds(img, 1), bass.ds(strip, 1), g].rearrange("a b s c f -> (a b s) c f")

    def stage(img, j, u, lag):
        if u >= lag or not (isinstance(j, int) and j == 0):
            if isinstance(img, int) and img >= B:
                return None
            return img, UNROLL * j + u - lag, (img * NJ + j) * UNROLL + u - lag
        if isinstance(img, int) and img == 0:
            return None
        return img - 1, NS + u - lag, (img * NJ + j) * UNROLL + u - lag

    def uses(img, j, v, slots):
        return (img * NJ + j) * (UNROLL // slots) + v // slots

    def steps(eng, body, last=UNROLL):
        def bodies(img, j):
            for u in range(UNROLL):
                body(img, j, u)

        def rest(img):
            if NJ > 1:
                with eng.Fori(1, NJ) as j:
                    bodies(img, j)

        bodies(0, 0)
        rest(0)
        with eng.Fori(1, B) as img:
            bodies(img, 0)
            rest(img)
        for u in range(last):
            body(B, 0, u)

    with ExitStack() as ctx:
        def sb(name, shape, dt=F32, where=ctx):
            return where.enter_context(nc.sbuf_tensor(name, shape, dt))

        def sem(name):
            return ctx.enter_context(nc.semaphore(name))

        psum = [ctx.enter_context(nc.psum_tensor(f"bank{i}", [P, 512], F32)) for i in range(8)]

        passed_sp, passed_act, passed_dve = sem("passed_sp"), sem("passed_act"), sem("passed_dve")
        group_avg = sb("group_avg", [P, P])
        ident = sb("ident", [P, P])
        vecs = sb("vecs", [P, 8])
        conv_bias, att_bias, out_bias, mlpw, mlpb, mapscale = (vecs[:, i:i + 1] for i in range(6))
        xn_scale, xn_bias, gate_scale, gate_bias = (sb(n, [P, B]) for n in ("xn_scale", "xn_bias", "gate_scale", "gate_bias"))
        x1_sums = sb("x1_sums", [P, 2, N])

        with ExitStack() as a:
            xa = sb("xa", [P, UNROLL, TILE], where=a)
            zeros = sb("zeros", [P, 2 * W], where=a)
            lowest = sb("lowest", [P, QUADS * W], where=a)
            bn = sb("bn", [P, NS * 4, 6], where=a)
            mv = sb("mv", [P, 2], where=a)
            moments = sb("moments", [P, B, 2], where=a)
            avg = sb("avg", [P, B, 2], where=a)
            tmp = sb("tmp", [P, 4, B], where=a)

            consts_loaded = sem("consts_loaded")
            a_loaded = [sem(f"a_loaded{u}") for u in range(UNROLL)]
            a_strips = sem("a_strips")
            a_mv = sem("a_mv")
            a_mean = sem("a_mean")
            a_square = sem("a_square")
            a_moments = sem("a_moments")
            a_avg = sem("a_avg")
            a_chain = sem("a_chain")
            a_std = sem("a_std")
            fills = sem("fills")
            edges = sem("edges")

            with nc.Block() as block:
                @block.sync
                def _(sp):
                    sp.dma_start(group_avg[:, :], same_group).then_inc(consts_loaded, 16)
                    sp.dma_start(ident[:, :], eye).then_inc(consts_loaded, 16)
                    for i, v in enumerate((conv_b, att_b, b1, mlp_w, mlp_b, map_scale)):
                        sp.dma_start(vecs[:, i:i + 1], v).then_inc(consts_loaded, 16)

                    def body(img, j, u):
                        got = stage(img, j, u, 0)
                        if got is None:
                            return
                        at, t, n = got
                        wait(sp, a_strips, n - UNROLL + 1)
                        passed(sp, passed_sp)
                        for g in range(2):
                            sp.dma_start(xa[:, u, 2 * W * g:2 * W * (g + 1)], strip_of(x, at, NS - 1 - t, g)).then_inc(a_loaded[u], 16)

                    steps(sp, body, 0)

                @block.gpsimd
                def _(pool):
                    pool.wait_ge(fills, 2)
                    for img in range(B):
                        for part in range(2):
                            for row in (0, H + HALO):
                                pool.dma_start(maps[part, img, row:row + HALO, :, :].rearrange("a m w -> a (m w)"),
                                               zeros[0:HALO, :]).then_inc(edges, 16)
                        pool.dma_start(below[img, :, NS].rearrange("c s w -> c (s w)"),
                                       lowest[0:C, :]).then_inc(edges, 16)
                    pool.wait_ge(edges, 16 * 5 * B)

                @block.tensor
                def _(pe):
                    pe.wait_ge(consts_loaded, 16 * 8)
                    pe.wait_ge(a_moments, B)
                    pe.matmul(psum[0][:, 0:2 * B], group_avg[:, :], moments[:, :, :].rearrange("p b k -> p (b k)"),
                              start=True, stop=True).then_inc(a_avg, 1)

                @block.scalar
                def _(act):
                    act.wait_ge(a_chain, 4)
                    act.activation(tmp[:, 1, :], tmp[:, 1, :], ACT.Sqrt).then_inc(a_std, 1)

                @block.vector
                def _(dve):
                    dve.memset(zeros[:, :], 0.0).then_inc(fills, 1)
                    dve.memset(lowest[:, :], LOWEST).then_inc(fills, 1)

                    def strips(img, j):
                        for u in range(UNROLL):
                            dve.wait_ge(a_loaded[u], 32 * (img * NJ + j + 1))
                            for k in range(4):
                                last = dve.bn_stats(bn[:, bass.ds((UNROLL * j + u) * 4 + k, 1), :].rearrange("p a k -> p (a k)"),
                                                    xa[:, u, k * W:(k + 1) * W])
                            last.then_inc(a_strips, 1)

                    with dve.Fori(0, B) as img:
                        with dve.Fori(0, NJ) as j:
                            strips(img, j)
                        dve.wait_ge(a_strips, (img + 1) * NS)
                        passed(dve, passed_dve)
                        dve.bn_aggr(mv[:, :], bn[:, :, :].rearrange("p a k -> p (a k)")).then_inc(a_mv, 1)
                        dve.wait_ge(a_mv, img + 1)
                        dve.tensor_copy(moments[:, bass.ds(img, 1), 0:1].rearrange("p a k -> p (a k)"), mv[:, 0:1]).then_inc(a_mean, 1)
                        dve.scalar_tensor_tensor(moments[:, bass.ds(img, 1), 1:2].rearrange("p a k -> p (a k)"), mv[:, 0:1], mv[:, 0:1],
                                                 mv[:, 1:2], ALU.mult, ALU.add).then_inc(a_moments, 1)
                        dve.wait_ge(a_moments, img + 1)
                        dve.wait_ge(a_mean, img + 1)
                    dve.wait_ge(a_avg, 1)
                    dve.tensor_copy(avg[:, :, :].rearrange("p b k -> p (b k)"), psum[0][:, 0:2 * B]).then_inc(a_chain, 1)
                    mean, square = avg[:, :, 0], avg[:, :, 1]
                    dve.wait_ge(a_chain, 1)
                    dve.tensor_tensor(tmp[:, 0, :], mean, mean, ALU.mult).then_inc(a_chain, 1)
                    dve.wait_ge(a_chain, 2)
                    dve.tensor_tensor(tmp[:, 1, :], square, tmp[:, 0, :], ALU.subtract).then_inc(a_chain, 1)
                    dve.wait_ge(a_chain, 3)
                    dve.tensor_scalar(tmp[:, 1, :], tmp[:, 1, :], 0.0, EPS, ALU.max, ALU.add).then_inc(a_chain, 1)
                    dve.wait_ge(a_std, 1)
                    dve.reciprocal(xn_scale[:, :], tmp[:, 1, :]).then_inc(a_chain, 1)
                    dve.wait_ge(a_chain, 5)
                    dve.scalar_tensor_tensor(xn_bias[:, :], mean, -1.0, xn_scale[:, :], ALU.mult, ALU.mult).then_inc(a_chain, 1)
                    dve.wait_ge(consts_loaded, 16 * 8)
                    dve.tensor_scalar(gate_scale[:, :], xn_scale[:, :], mlpw, None, ALU.mult).then_inc(a_chain, 1)
                    dve.wait_ge(a_chain, 7)
                    dve.tensor_scalar(tmp[:, 2, :], xn_bias[:, :], mlpw, 2.0, ALU.mult, ALU.mult).then_inc(a_chain, 1)
                    dve.tensor_scalar(tmp[:, 3, 0:1], mlpb, 2.0, None, ALU.mult).then_inc(a_chain, 1)
                    dve.wait_ge(a_chain, 9)
                    dve.tensor_scalar(gate_bias[:, :], tmp[:, 2, :], tmp[:, 3, 0:1], None, ALU.add).then_inc(a_chain, 1)
                    dve.wait_ge(a_chain, 10)

        with ExitStack() as b:
            wg = sb("wg", [P, P], where=b)
            wp = sb("wp", [P, P], where=b)
            wa = sb("wa", [KCONV, 2, 2, 2, P], F32R, where=b)
            xs = sb("xs", [P, UNROLL, TILE], where=b)
            xn = sb("xn", [P, 2, TILE], where=b)
            gated = sb("gated", [P, 2, TILE], where=b)
            fs = sb("fs", [P, 4, TILE], where=b)
            att = sb("att", [P, 2, TILE], where=b)
            win = sb("win", [KCONV, 2, 2, 2, W + 4], F32R, where=b)
            pair_max = sb("pair_max", [P, 2, W], where=b)
            below_pair = sb("below_pair", [P, 2, W], where=b)
            pool_max = sb("pool_max", [P, 2, W // 2], where=b)
            gate_in = sb("gate_in", [P, 2, 2, W // 2], where=b)
            pair_sum = sb("pair_sum", [P, 2, W], where=b)
            pool_sum = sb("pool_sum", [P, 2, 2, W // 2], where=b)
            gate = sb("gate", [P, 2, 2, W // 2], where=b)
            run_max = sb("run_max", [P, 2, W], where=b)
            map_cols = sb("map_cols", [P, 2, P], where=b)
            map_rows = sb("map_rows", [P, 2, 2, P], F32R, where=b)
            wa_full = fs[0:KCONV, 3, 0:4 * P].rearrange("p (r h m) -> p r h m", r=2, h=2)
            unused = sb("unused", [P, TILE], BF16, where=b)

            names = ("weights_loaded map_lows wa_highs wa_lows x_pair_sums pool_sums pair_maxes pool_maxes gate_ins xns gates gateds "
                     "out_rows fs_rows reduced transposed map_rows_ready att_rows sig_rows products x1s "
                     "below_pairs below_rows below_ready sums_taken win_cleared").split()
            s_ = {k: sem(k) for k in names}
            x_loaded = [sem(f"x_loaded{u}") for u in range(UNROLL)]
            x1_stored = [sem(f"x1_stored{u}") for u in range(UNROLL)]
            maps_stored = [sem(f"maps_stored{u}") for u in range(2)]
            below_stored = [sem(f"below_stored{u}") for u in range(2)]
            win_loaded = [sem(f"win_loaded{u}") for u in range(2)]
            (weights_loaded, map_lows, wa_highs, wa_lows, x_pair_sums, pool_sums, pair_maxes, pool_maxes, gate_ins, xns, gates, gateds,
             out_rows, fs_rows, reduced, transposed, map_rows_ready, att_rows, sig_rows, products, x1s,
             below_pairs, below_rows, below_ready, sums_taken, win_cleared) = (s_[k] for k in names)

            def grw(tile):
                return tile.rearrange("p (g r w) -> p g r w", g=2, r=2)

            att_bank = (4, 5, 6, 4)
            att_bank_read = (0, -2, -1, 1)
            ROWS = 4
            map_psum = [psum[7][:, P * k:P * (k + 1)] for k in range(2)]
            passes = [(half, wpart, part) for wpart, part in ((0, 1), (1, 0), (0, 0)) for half in range(2)]

            with nc.Block() as block:
                @block.sync
                def _(sp):
                    sp.dma_start(wg[:, :], w_gated).then_inc(weights_loaded, 16)
                    sp.dma_start(wp[:, :], w_plain).then_inc(weights_loaded, 16)
                    for k in range(2):
                        sp.sem_inc(below_stored[k], 1)
                    sp.dma_start(wa_full, w_att).then_inc(weights_loaded, 16)

                    def body(img, j, u):
                        if got := stage(img, j, u, 4):
                            at, t, n = got
                            wait(sp, map_rows_ready, n + 1)
                            wait(sp, map_lows, n + 1)
                            passed(sp, passed_sp)
                            k = n_slot(u, 4)
                            for g in range(2):
                                row = HALO + STRIP * (NS - 1 - t) + 8 * g
                                for part in range(2):
                                    rows = maps[part, bass.ds(at, 1), bass.ds(row, 8)].rearrange(
                                        "a (s r) m (k w) -> (a r m k) s w", s=QUADS, w=LANES)
                                    sp.dma_start(rows, map_rows[64 * g:64 * (g + 1), k, part, :].bitcast(F32).rearrange(
                                        "p (s w) -> p s w", s=QUADS)).then_inc(maps_stored[k], 16)
                        if got := stage(img, j, u, 0):
                            at, t, n = got
                            it = img * NJ + j
                            wait(sp, x1_stored[u], 32 * it)
                            passed(sp, passed_sp)
                            wait(sp, sums_taken, 2 * (n - UNROLL + 1))
                            wait(sp, below_pairs, n - UNROLL + 1)
                            passed(sp, passed_sp)
                            for g in range(2):
                                sp.dma_start(xs[:, u, 2 * W * g:2 * W * (g + 1)], strip_of(x, at, NS - 1 - t, g)).then_inc(x_loaded[u], 16)
                        if got := stage(img, j, u, 5):
                            at, t, n = got
                            if isinstance(n, int) and n == N - 1:
                                sp.wait_ge(maps_stored[n % 2], 64 * (N // 2))
                            else:
                                sp.wait_ge(maps_stored[n_slot(u, 4)], 64 * (uses(img, j, u - 4, 2) + 1))
                            passed(sp, passed_sp)
                            wait(sp, att_rows, ROWS * (n - 1))
                            passed(sp, passed_sp)
                            for k in range(COLTAPS):
                                row = STRIP * (NS - 1 - t)
                                for g in range(2):
                                    sp.dma_start(
                                        win[2 * WIN * k:2 * WIN * (k + 1), n_slot(u, 5), g, :, HALO - k:HALO - k + W].bitcast(F32),
                                        maps[:, bass.ds(at, 1), bass.ds(row + 8 * g, WIN)].rearrange("e a r m w -> (a r m) e w")
                                    ).then_inc(win_loaded[n_slot(u, 5)], 16)
                        if got := stage(img, j, u, 7):
                            at, t, n = got
                            wait(sp, x1s, n + 1)
                            passed(sp, passed_sp)
                            v = (u - 7) % UNROLL
                            for g in range(2):
                                sp.dma_start(strip_of(x1, at, NS - 1 - t, g), xs[:, v, 2 * W * g:2 * W * (g + 1)]).then_inc(x1_stored[v], 16)
                        if got := stage(img, j, u, 8):
                            at, t, n = got
                            wait(sp, below_ready, n + 1)
                            passed(sp, passed_sp)
                            dst = below[bass.ds(at, 1), :, bass.ds(NS - 1 - t, 1)].rearrange("a c n s w -> s (a c n) w")
                            sp.dma_start(dst, run_max[:, n_slot(u, 8), :]).then_inc(below_stored[n_slot(u, 8)], 16)

                    def n_slot(u, lag, slots=2):
                        return (u - lag) % slots

                    steps(sp, body)
                    for v in range(UNROLL):
                        sp.wait_ge(x1_stored[v], 32 * (N // UNROLL))
                    for k in range(2):
                        sp.wait_ge(below_stored[k], 16 * (N // 2) + 1)
                        sp.wait_ge(maps_stored[k], 64 * (N // 2))

                @block.gpsimd
                def _(pool):
                    def body(img, j, u):
                        if got := stage(img, j, u, 0):
                            _, _, n = got
                            it = img * NJ + j
                            rows = grw(xs[:, u, :])
                            pool.wait_ge(x_loaded[u], 32 * (it + 1))
                            wait(pool, pool_sums, n)
                            pool.tensor_tensor(pair_sum[:, :, :], rows[:, :, 0], rows[:, :, 1], ALU.add).then_inc(x_pair_sums, 1)
                            pool.wait_ge(x_pair_sums, n + 1)
                            wait(pool, gate_ins, n - 1)
                            pairs = pair_sum[:, :, :].rearrange("p g (w d) -> p g w d", d=2)
                            pool.tensor_tensor(pool_sum[:, u % 2], pairs[:, :, :, 0], pairs[:, :, :, 1], ALU.add).then_inc(pool_sums, 1)
                        if got := stage(img, j, u, 1):
                            _, _, n = got
                            k = (u - 1) % 2
                            pool.wait_ge(gates, n + 1)
                            pool.wait_ge(xns, n + 1)
                            wait(pool, out_rows, ROWS * (n - 1))
                            for g in range(2):
                                src = grw(xn[:, k, :])[:, g].rearrange("p r (w d) -> p r w d", d=2)
                                dst = grw(gated[:, k, :])[:, g].rearrange("p r (w d) -> p r w d", d=2)
                                by = gate[:, k, g, :].unsqueeze(1).unsqueeze(3).broadcast_to([P, 2, W // 2, 2])
                                last = pool.tensor_tensor(dst, src, by, ALU.mult)
                            last.then_inc(gateds, 1)
                        if got := stage(img, j, u, 6):
                            _, _, n = got
                            v = (u - 6) % UNROLL
                            pool.wait_ge(products, n + 1)
                            pool.tensor_tensor(xs[:, v, :], xs[:, v, :], att[:, (u - 6) % 2, :], ALU.add).then_inc(x1s, 1)

                    steps(pool, body)

                @block.scalar
                def _(act):
                    def stats(k, f, n, v):
                        act.wait_ge(x1s, n + 1)
                        wait(act, sums_taken, 2 * n + k)
                        passed(act, passed_act)
                        act.activation(unused[:, :], xs[:, v, :], f, accum_out=x1_sums[:, k, bass.ds(n, 1)]).then_inc(sums_taken, 1)

                    def sigmoids(rows, n, k):
                        wait(act, x1s, n - 1)
                        for q in rows:
                            act.wait_ge(att_rows, ROWS * n + q + 1)
                            act.activation(att[:, k, q * W:(q + 1) * W], psum[att_bank[q]][:, 0:W],
                                           ACT.Sigmoid, bias=att_bias).then_inc(sig_rows, 1)

                    def body(img, j, u):
                        if got := stage(img, j, u, 1):
                            at, _, n = got
                            it = uses(img, j, u - 1, UNROLL)
                            act.wait_ge(x_loaded[(u - 1) % UNROLL], 32 * (it + 1))
                            wait(act, out_rows, ROWS * (n - 1))
                            passed(act, passed_act)
                            act.activation(xn[:, (u - 1) % 2, :], xs[:, (u - 1) % UNROLL, :], ACT.Identity, scale=xn_scale[:, bass.ds(at, 1)],
                                           bias=xn_bias[:, bass.ds(at, 1)]).then_inc(xns, 1)
                        if got := stage(img, j, u, 1):
                            at, _, n = got
                            k = (u - 1) % 2
                            act.wait_ge(gate_ins, n + 1)
                            wait(act, gateds, n - 1)
                            passed(act, passed_act)
                            act.activation(gate[:, k], gate_in[:, k], ACT.Sigmoid,
                                           scale=gate_scale[:, bass.ds(at, 1)], bias=gate_bias[:, bass.ds(at, 1)]).then_inc(gates, 1)
                        if got := stage(img, j, u, 2):
                            _, _, n = got
                            wait(act, products, n - 3)
                            for q in range(ROWS):
                                act.wait_ge(out_rows, ROWS * n + q + 1)
                                act.activation(fs[:, (u - 2) % 4, q * W:(q + 1) * W], psum[q][:, 0:W], ACT.Identity,
                                               bias=conv_bias).then_inc(fs_rows, 1)
                        if got := stage(img, j, u, 3):
                            _, _, n = got
                            act.wait_ge(transposed, n + 1)
                            wait(act, map_lows, n - 1)
                            wait(act, maps_stored[(u - 3) % 2], 64 * uses(img, j, u - 3, 2))
                            act.activation(map_rows[:, (u - 3) % 2, 0, :], map_psum[(u - 3) % 2], ACT.Identity,
                                           scale=mapscale).then_inc(map_rows_ready, 1)
                        if got := stage(img, j, u, 7):
                            stats(0, ACT.Identity, got[2], (u - 7) % UNROLL)
                        if got := stage(img, j, u, 5):
                            sigmoids(range(0, 1), got[2], (u - 5) % 2)
                        if got := stage(img, j, u, 7):
                            stats(1, ACT.Square, got[2], (u - 7) % UNROLL)
                        if got := stage(img, j, u, 5):
                            sigmoids(range(1, 4), got[2], (u - 5) % 2)

                    steps(act, body)

                @block.vector
                def _(dve):
                    dve.memset(win[:, :, :, :, :].bitcast(F32), 0.0).then_inc(win_cleared, 1)
                    dve.wait_ge(weights_loaded, 48)
                    dve.tensor_copy(wa[:, 0], wa_full).then_inc(wa_highs, 1)
                    dve.wait_ge(wa_highs, 1)
                    dve.tensor_tensor(wa[:, 1], wa_full, wa[:, 0].bitcast(F32), ALU.subtract).then_inc(wa_lows, 1)

                    def body(img, j, u):
                        lows_now = stage(img, j, u, 3)
                        maps_now, out_now = stage(img, j, u, 3), stage(img, j, u, 6)
                        pool_now, below_now = stage(img, j, u, 0), stage(img, j, u, 7)
                        if maps_now:
                            _, _, o = maps_now
                            dve.wait_ge(fs_rows, ROWS * (o + 1))
                            wait(dve, transposed, o - 1)
                            cols = map_cols[:, (u - 3) % 2, :].rearrange("p (q m k) -> p q m k", m=2, k=WB)
                            src = fs[:, (u - 3) % 4, :].rearrange("p (q k c) -> p q k c", q=ROWS, c=LANES)
                            for m, op in enumerate((ALU.max, ALU.add)):
                                dve.tensor_reduce(cols[:, :, m, :], src, AX_X, op, apply_transpose=True).then_inc(reduced, 1)
                        if out_now:
                            _, _, p = out_now
                            dve.wait_ge(sig_rows, ROWS * (p + 1))
                            dve.tensor_tensor(att[:, (u - 6) % 2, :], att[:, (u - 6) % 2, :], fs[:, (u - 6) % 4, :],
                                              ALU.mult).then_inc(products, 1)
                        if pool_now:
                            _, _, n = pool_now
                            rows = grw(xs[:, u, :])
                            dve.wait_ge(x_loaded[u], 32 * (uses(img, j, u, UNROLL) + 1))
                            dve.tensor_tensor(pair_max[:, :, :], rows[:, :, 0], rows[:, :, 1], ALU.max).then_inc(pair_maxes, 1)
                        if below_now:
                            _, t_below, b = below_now
                            k = (u - 7) % 2
                            rows = grw(xs[:, (u - 7) % UNROLL, :])
                            first = isinstance(t_below, int) and t_below == 0
                            dve.wait_ge(x1s, b + 1)
                            wait(dve, below_ready, b)
                            dve.tensor_tensor(below_pair[:, :, :], rows[:, :, 0], rows[:, :, 1], ALU.max).then_inc(below_pairs, 1)
                        if lows_now:
                            _, _, m = lows_now
                            k = (u - 3) % 2
                            dve.wait_ge(map_rows_ready, m + 1)
                            wait(dve, maps_stored[k], 64 * uses(img, j, u - 3, 2))
                            dve.scalar_tensor_tensor(map_rows[:, k, 1, :], map_psum[k], mapscale, map_rows[:, k, 0, :].bitcast(F32),
                                                     ALU.mult, ALU.subtract).then_inc(map_lows, 1)
                        if pool_now:
                            dve.wait_ge(pair_maxes, n + 1)
                            wait(dve, gate_ins, n)
                            pairs = pair_max[:, :, :].rearrange("p g (w d) -> p g w d", d=2)
                            dve.tensor_tensor(pool_max[:, :, :], pairs[:, :, :, 0], pairs[:, :, :, 1], ALU.max).then_inc(pool_maxes, 1)
                        if below_now:
                            dve.wait_ge(below_pairs, b + 1)
                            dve.wait_ge(below_stored[k], 16 * uses(img, j, u - 7, 2) + 1)
                            dve.tensor_tensor(run_max[:, k, :], below_pair[:, 0, :], below_pair[:, 1, :],
                                              ALU.max).then_inc(below_rows, 1)
                        if pool_now:
                            dve.wait_ge(pool_maxes, n + 1)
                            dve.wait_ge(pool_sums, n + 1)
                            wait(dve, gates, n - 1)
                            dve.scalar_tensor_tensor(gate_in[:, u % 2], pool_sum[:, u % 2], 0.25, pool_max[:, :, :],
                                                     ALU.mult, ALU.add).then_inc(gate_ins, 1)
                        if below_now:
                            dve.wait_ge(below_rows, b + 1)
                            wait(dve, below_ready, b)
                            if first:
                                dve.tensor_scalar(run_max[:, k, :], run_max[:, k, :], LOWEST, None, ALU.max).then_inc(below_ready, 1)
                            else:
                                dve.tensor_tensor(run_max[:, k, :], run_max[:, k, :], run_max[:, 1 - k, :],
                                                  ALU.max).then_inc(below_ready, 1)

                    steps(dve, body)

                @block.tensor
                def _(pe):
                    pe.wait_ge(weights_loaded, 48)
                    pe.wait_ge(wa_lows, 1)

                    def body(img, j, u):
                        if got := stage(img, j, u, 0):
                            _, _, n = got
                            pe.wait_ge(xns, n + 1)
                            for q in range(ROWS):
                                wait(pe, fs_rows, ROWS * (n - 1) + q + 1)
                                pe.matmul(psum[q][:, 0:W], wp[:, :], xn[:, u % 2, q * W:(q + 1) * W], start=True, stop=False)
                            pe.wait_ge(gateds, n + 1)
                            for q in range(ROWS):
                                pe.matmul(psum[q][:, 0:W], wg[:, :], gated[:, u % 2, q * W:(q + 1) * W],
                                          start=False, stop=True).then_inc(out_rows, 1)
                        if got := stage(img, j, u, 1):
                            _, _, n = got
                            pe.wait_ge(reduced, 2 * (n + 1))
                            wait(pe, map_lows, n - 1)
                            pe.transpose(map_psum[(u - 1) % 2], map_cols[:, (u - 1) % 2, :], ident[:, :]).then_inc(transposed, 1)
                        if got := stage(img, j, u, 3):
                            _, _, n = got
                            k = (u - 3) % 2
                            pe.wait_ge(win_loaded[k], 16 * 2 * COLTAPS * (uses(img, j, u - 3, 2) + 1))
                            for q in range(ROWS):
                                g, r = divmod(q, 2)
                                wait(pe, sig_rows, ROWS * n + att_bank_read[q])
                                for at, (half, wpart, part) in enumerate(passes):
                                    last = pe.matmul(psum[att_bank[q]][:, 0:W], wa[:, wpart, r, half, :],
                                                     win[:, k, g, part, COLTAPS * half:COLTAPS * half + W],
                                                     start=(at == 0), stop=(at == len(passes) - 1))
                                last.then_inc(att_rows, 1)

                    steps(pe, body)

        with ExitStack() as c:
            w_raw = sb("w_raw", [P, 5, P], where=c)
            w_now = sb("w_now", [P, 5, P], where=c)
            spread = sb("spread", [P, 2, P], where=c)
            share = sb("share", [P, 1], where=c)
            sums = sb("sums", [P, 2, B], where=c)
            st = sb("st", [P, 8], where=c)
            xt = sb("xt", [P, 2, STRIP, W], where=c)
            up = sb("up", [P, 2, STRIP, W], where=c)
            down = sb("down", [P, 2 * SUB, W], where=c)
            right = sb("right", [P, 2 * SUB, W], where=c)
            left = sb("left", [P, 2 * SUB, W], where=c)
            yt = sb("yt", [P, 2, SUB, W], where=c)
            w_high = sb("w_high", [P, 2, P], F32R, where=c)
            w_low = sb("w_low", [P, 2, P], F32R, where=c)
            x_high = sb("x_high", [P, 2, SUB, W], F32R, where=c)
            x_low = sb("x_low", [P, 2, SUB, W], F32R, where=c)
            up_high = sb("up_high", [P, 2, SUB, W], F32R, where=c)
            up_low = sb("up_low", [P, 2, SUB, W], F32R, where=c)

            names = ("c_weights summed spread_ready set_moments c_chain c_std c_scaled bias_mm set_ready bl_max "
                     "up_rows down_rows right_rows left_rows y_rows y_out y_stored0 y_stored1 top_cleared "
                     "w_full w_highs x_highs x_lows up_highs up_lows").split()
            s_ = {k: sem(k) for k in names}
            (c_weights, summed, spread_ready, set_moments, c_chain, c_std, c_scaled, bias_mm, set_ready, bl_max,
             up_rows, down_rows, right_rows, left_rows, y_rows, y_out, y_stored0, y_stored1, top_cleared,
             w_full, w_highs, x_highs, x_lows, up_highs, up_lows) = (s_[k] for k in names)
            y_stored = (y_stored0, y_stored1)
            bl_loaded = [sem(f"bl_loaded{k}") for k in range(2)]
            x1_loaded = [[sem(f"c_loaded{k}_{p}") for p in range(4)] for k in range(2)]
            QROWS = STRIP // 4
            RING = 2 * SUB
            NT = SETS * NS

            def piece_of(g, i, q):
                if q < 0:
                    i, q = i - 1, q + 2 * PIECES
                return (g, i) + divmod(q, PIECES)

            def pieces(eng, g, body):
                def pair(i, first):
                    for q in range(2 * PIECES):
                        body(g, i, q, first)

                pair(0, True)
                if NS > 2:
                    with eng.Fori(1, NS // 2) as i:
                        pair(i, False)

            x1_v = x1.rearrange("b c h w -> (b c) h w")
            y_v = y.rearrange("b c h w -> (b c) h w")
            below_v = below.rearrange("b c n s w -> (b c) n s w")

            with nc.Block() as block:
                @block.sync
                def _(sp):
                    sp.dma_start(w_raw[:, :, :], w1).then_inc(c_weights, 16)

                    def load(g, i, k):
                        tile, n = 2 * i + k, NS * g + 2 * i + k
                        for q in range(4):
                            wait(sp, y_rows, STRIP * (n - 2) + QROWS * (q + 1))
                            passed(sp, passed_sp)
                            sp.dma_start(xt[:, k, QROWS * q:QROWS * (q + 1), :],
                                         x1_v[bass.ds(P * g, P), bass.ds(STRIP * tile + QROWS * q, QROWS)]
                                         ).then_inc(x1_loaded[k][q], 16)
                        sp.dma_start(up[:, k, 0:QUADS, :], below_v[bass.ds(P * g, P), bass.ds(tile + 1, 1)].rearrange(
                            "p n s w -> p (n s) w")).then_inc(bl_loaded[k], 16)

                    for k in range(2):
                        load(0, 0, k)
                    if NS > 2:
                        with sp.Fori(1, NS // 2) as i:
                            for k in range(2):
                                load(0, i, k)
                    with sp.Fori(1, SETS) as g:
                        with sp.Fori(0, NS // 2) as i:
                            for k in range(2):
                                load(g, i, k)

                @block.gpsimd
                def _(pool):
                    def subtract(g, i, k, p):
                        m = PIECES * (NS * g + 2 * i + k) + p
                        rows = slice(SUB * p, SUB * (p + 1))
                        pool.wait_ge(x_highs, m + 1)
                        pool.tensor_tensor(x_low[:, p % 2], xt[:, k, rows, :], x_high[:, p % 2].bitcast(F32),
                                           ALU.subtract).then_inc(x_lows, 1)
                        pool.wait_ge(up_highs, m + 1)
                        pool.tensor_tensor(up_low[:, p % 2], up[:, k, rows, :], up_high[:, p % 2].bitcast(F32),
                                           ALU.subtract).then_inc(up_lows, 1)

                    def store(g, i, k, p):
                        tile, n = 2 * i + k, NS * g + 2 * i + k
                        pool.wait_ge(y_out, STRIP * n + SUB * (p + 1))
                        pool.dma_start(y_v[bass.ds(P * g, P), bass.ds(STRIP * tile + SUB * p, SUB)],
                                       yt[:, p % 2]).then_inc(y_stored[p % 2], 16)

                    def body(g, i, q, first):
                        subtract(*piece_of(g, i, q))
                        if not first or q >= LAG:
                            store(*piece_of(g, i, q - LAG))

                    LAG = 2
                    def whole(g):
                        pieces(pool, g, body)
                        for q in range(2 * PIECES - LAG, 2 * PIECES):
                            store(*piece_of(g, NS // 2 - 1, q))

                    whole(0)
                    with pool.Fori(1, SETS) as g:
                        whole(g)
                    for v in range(2):
                        pool.wait_ge(y_stored[v], 16 * NT * (PIECES // 2))

                @block.scalar
                def _(act):
                    def split(g, i, k, p):
                        n = NS * g + 2 * i + k
                        rows = slice(SUB * p, SUB * (p + 1))
                        wait(act, y_rows, SUB * (PIECES * n + p - 1))
                        if SUB * p % QROWS == 0:
                            act.wait_ge(x1_loaded[k][SUB * p // QROWS], 16 * ((NS // 2) * g + i + 1))
                        act.activation(x_high[:, p % 2], xt[:, k, rows, :], ACT.Identity).then_inc(x_highs, 1)
                        if p == 0:
                            act.wait_ge(up_rows, STRIP * (n + 1))
                        act.activation(up_high[:, p % 2], up[:, k, rows, :], ACT.Identity).then_inc(up_highs, 1)

                    def emit(g, i, k, p):
                        n = NS * g + 2 * i + k
                        wait(act, y_stored[p % 2], 16 * (PIECES // 2 * n + p // 2))
                        for h in range(SUB * p, SUB * (p + 1)):
                            act.wait_ge(y_rows, STRIP * n + h + 1)
                            act.activation(yt[:, p % 2, h % SUB, :], psum[h % 4][:, 0:W], ACT.Identity,
                                           bias=st[:, 6:7]).then_inc(y_out, 1)

                    def body(g, i, q, first):
                        split(*piece_of(g, i, q))
                        if not first or q >= 1:
                            emit(*piece_of(g, i, q - 1))

                    def prepare(g):
                        act.wait_ge(c_chain, 5 * g + 4)
                        act.activation(st[:, 2:3], st[:, 2:3], ACT.Sqrt).then_inc(c_std, 1)
                        act.wait_ge(set_ready, 3 * (g + 1))

                    def whole(g):
                        prepare(g)
                        pieces(act, g, body)
                        emit(*piece_of(g, NS // 2 - 1, 2 * PIECES - 1))

                    whole(0)
                    with act.Fori(1, SETS) as g:
                        whole(g)

                @block.tensor
                def _(pe):
                    def prepare(g):
                        pe.wait_ge(spread_ready, 8 * (g + 1))
                        for k in range(2):
                            last = pe.matmul(psum[4][:, k:k + 1], spread[:, k, :], share[:, :], start=True, stop=True)
                        last.then_inc(set_moments, 1)
                        pe.wait_ge(c_scaled, 5 * (g + 1))
                        for k in range(5):
                            last = pe.matmul(psum[5][:, 0:1], w_now[:, k, :], st[:, 5:6], start=(k == 0), stop=(k == 4))
                        last.then_inc(bias_mm, 1)
                        pe.wait_ge(set_ready, 3 * (g + 1))

                    def multiply(g, i):
                        for k in range(2):
                            n = NS * g + 2 * i + k
                            for h in range(STRIP):
                                row = STRIP * n + h
                                bank = psum[h % 4][:, 0:W]
                                wait(pe, y_out, row - 3)
                                piece, slot, r = h // SUB, h // SUB % 2, h % SUB
                                if r == 0:
                                    pe.wait_ge(x_lows, PIECES * n + piece + 1)
                                    pe.wait_ge(up_lows, PIECES * n + piece + 1)
                                pe.matmul(bank, w_high[:, 0, :], x_low[:, slot, r, :], start=True, stop=False)
                                pe.matmul(bank, w_low[:, 0, :], x_high[:, slot, r, :], start=False, stop=False)
                                pe.matmul(bank, w_high[:, 0, :], x_high[:, slot, r, :], start=False, stop=False)
                                pe.matmul(bank, w_high[:, 1, :], up_low[:, slot, r, :], start=False, stop=False)
                                pe.matmul(bank, w_low[:, 1, :], up_high[:, slot, r, :], start=False, stop=False)
                                pe.matmul(bank, w_high[:, 1, :], up_high[:, slot, r, :], start=False, stop=False)
                                pe.wait_ge(down_rows, row + 1)
                                pe.matmul(bank, w_now[:, 1, :], down[:, h % RING, :], start=False, stop=False)
                                pe.wait_ge(right_rows, row + 1)
                                pe.matmul(bank, w_now[:, 3, :], right[:, h % RING, :], start=False, stop=False)
                                pe.wait_ge(left_rows, row + 1)
                                pe.matmul(bank, w_now[:, 4, :], left[:, h % RING, :], start=False, stop=True).then_inc(y_rows, 1)

                    prepare(0)
                    multiply(0, 0)
                    if NS > 2:
                        with pe.Fori(1, NS // 2) as i:
                            multiply(0, i)
                    with pe.Fori(1, SETS) as g:
                        prepare(g)
                        with pe.Fori(0, NS // 2) as i:
                            multiply(g, i)

                @block.vector
                def _(dve):
                    dve.memset(share[:, :], QUADS * GROUP / (GROUP * HW)).then_inc(summed, 1)
                    for k in range(2):
                        dve.tensor_reduce(sums[:, k, :], x1_sums[:, k, :].rearrange("p (b n) -> p b n", n=NS), AX_X,
                                          ALU.add).then_inc(summed, 1)
                    dve.wait_ge(summed, 3)
                    dve.wait_ge(c_weights, 16)

                    def prepare(g):
                        wait(dve, y_rows, STRIP * NS * g)
                        wait(dve, y_out, STRIP * NS * g)
                        for k in range(2):
                            for a in range(SET):
                                dve.tensor_scalar(spread[:, k, LANES * a:LANES * (a + 1)], group_avg[:, 0:LANES],
                                                  sums[:, k, bass.ds(SET * g + a, 1)], None, ALU.mult).then_inc(spread_ready, 1)
                        dve.wait_ge(set_moments, g + 1)
                        dve.tensor_copy(st[:, 0:2], psum[4][:, 0:2]).then_inc(c_chain, 1)
                        dve.wait_ge(c_chain, 5 * g + 1)
                        dve.tensor_scalar(st[:, 5:6], st[:, 0:1], -1.0, None, ALU.mult).then_inc(c_chain, 1)
                        dve.wait_ge(c_chain, 5 * g + 2)
                        dve.scalar_tensor_tensor(st[:, 2:3], st[:, 0:1], st[:, 5:6], st[:, 1:2], ALU.mult, ALU.add).then_inc(c_chain, 1)
                        dve.wait_ge(c_chain, 5 * g + 3)
                        dve.tensor_scalar(st[:, 2:3], st[:, 2:3], 0.0, EPS, ALU.max, ALU.add).then_inc(c_chain, 1)
                        dve.wait_ge(c_std, g + 1)
                        dve.reciprocal(st[:, 3:4], st[:, 2:3]).then_inc(c_chain, 1)
                        dve.wait_ge(c_chain, 5 * g + 5)
                        for k in range(5):
                            dve.tensor_scalar(w_now[:, k, :], w_raw[:, k, :], st[:, 3:4], None, ALU.mult).then_inc(c_scaled, 1)
                        dve.wait_ge(bias_mm, g + 1)
                        dve.tensor_tensor(st[:, 6:7], psum[5][:, 0:1], out_bias, ALU.add).then_inc(set_ready, 1)
                        dve.tensor_tensor(w_now[:, 0, :], w_now[:, 0, :], ident[:, :], ALU.add).then_inc(w_full, 1)
                        dve.wait_ge(w_full, g + 1)
                        for at, k in enumerate((0, 2)):
                            dve.tensor_copy(w_high[:, at, :], w_now[:, k, :]).then_inc(w_highs, 1)
                        for at, k in enumerate((0, 2)):
                            dve.wait_ge(w_highs, 2 * g + at + 1)
                            dve.tensor_tensor(w_low[:, at, :], w_now[:, k, :], w_high[:, at, :].bitcast(F32),
                                              ALU.subtract).then_inc(set_ready, 1)
                        dve.memset(down[:, RING - 1, :], LOWEST).then_inc(top_cleared, 1)
                        dve.wait_ge(top_cleared, g + 1)

                    def up_start(g, i, k, n):
                        dve.wait_ge(bl_loaded[k], 16 * ((NS // 2) * g + i + 1))
                        dve.tensor_tensor(up[:, k, 0, :], up[:, k, 0, :], up[:, k, 1, :], ALU.max).then_inc(bl_max, 1)
                        dve.tensor_tensor(up[:, k, 2, :], up[:, k, 2, :], up[:, k, 3, :], ALU.max).then_inc(bl_max, 1)
                        dve.wait_ge(bl_max, 3 * n + 2)
                        dve.tensor_tensor(up[:, k, 0, :], up[:, k, 0, :], up[:, k, 2, :], ALU.max).then_inc(bl_max, 1)

                    def up_row(g, i, k, n, h):
                        if h % QROWS == QROWS - 1:
                            dve.wait_ge(x1_loaded[k][h // QROWS], 16 * ((NS // 2) * g + i + 1))
                        if h == STRIP - 1:
                            dve.wait_ge(bl_max, 3 * n + 3)
                            dve.tensor_tensor(up[:, k, h, :], xt[:, k, h, :], up[:, k, 0, :], ALU.max).then_inc(up_rows, 1)
                        else:
                            dve.wait_ge(up_rows, STRIP * n + STRIP - 1 - h)
                            dve.tensor_tensor(up[:, k, h, :], xt[:, k, h, :], up[:, k, h + 1, :], ALU.max).then_inc(up_rows, 1)

                    def row(k, n, h):
                        at = STRIP * n + h
                        ring = h % RING
                        src = xt[:, k, h, :]
                        wait(dve, y_rows, at - RING + 1)
                        if isinstance(at, int) and at == 0:
                            pass
                        else:
                            dve.wait_ge(down_rows, at)
                        dve.tensor_tensor(down[:, ring, :], src, down[:, (ring - 1) % RING, :], ALU.max).then_inc(down_rows, 1)
                        dve.tensor_tensor_scan(right[:, ring, :], src, src, LOWEST, ALU.max, ALU.max).then_inc(right_rows, 1)
                        dve.tensor_tensor_scan(left[:, ring, ::-1], src[:, ::-1], src[:, ::-1], LOWEST, ALU.max, ALU.max).then_inc(left_rows, 1)

                    def tile(g, i, k, following):
                        n = NS * g + 2 * i + k
                        for h in range(STRIP):
                            row(k, n, h)
                            if following and h >= STRIP // 2:
                                fg, fi, fk = following
                                if h == STRIP // 2:
                                    up_start(fg, fi, fk, n + 1)
                                for e in range(2):
                                    up_row(fg, fi, fk, n + 1, STRIP - 1 - 2 * (h - STRIP // 2) - e)

                    def whole(g):
                        prepare(g)
                        up_start(g, 0, 0, NS * g)
                        for h in range(STRIP - 1, -1, -1):
                            up_row(g, 0, 0, NS * g, h)

                    whole(0)
                    tile(0, 0, 0, (0, 0, 1))
                    if NS > 2:
                        tile(0, 0, 1, (0, 1, 0))
                        if NS > 4:
                            with dve.Fori(1, NS // 2 - 1) as i:
                                tile(0, i, 0, (0, i, 1))
                                tile(0, i, 1, (0, i + 1, 0))
                        tile(0, NS // 2 - 1, 0, (0, NS // 2 - 1, 1))
                    tile(0, NS // 2 - 1, 1, None)
                    with dve.Fori(1, SETS) as g:
                        whole(g)
                        if NS > 2:
                            with dve.Fori(0, NS // 2 - 1) as i:
                                tile(g, i, 0, (g, i, 1))
                                tile(g, i, 1, (g, i + 1, 0))
                        tile(g, NS // 2 - 1, 0, (g, NS // 2 - 1, 1))
                        tile(g, NS // 2 - 1, 1, None)


def blocks(w):
    out = np.zeros((QUADS, LANES, QUADS, LANES), w.dtype)
    for s in range(QUADS):
        out[s, :, s, :] = w.T
    return out.reshape(P, P)


def attention_blocks(w):
    out = np.zeros((COLTAPS, WIN, 2, 2, 2, QUADS, LANES), w.dtype)
    for half in range(2):
        for k in range(COLTAPS):
            j = COLTAPS * half + k
            if j < TAPS:
                for r in range(2):
                    for s in range(QUADS):
                        for i in range(TAPS):
                            out[k, 2 * s + r + i, :, r, half, s, :] = w[:, :, i, j].T
    return out.reshape(KCONV, 2, 2, P)


def layout(v):
    C = v["x"].shape[1]
    tile = lambda a: np.ascontiguousarray(np.tile(np.asarray(a).reshape(-1), P // np.asarray(a).size).reshape(P, 1))
    lane = np.arange(P) % LANES // GROUP
    same = (lane[:, None] == lane[None, :]).astype(np.float32) / (QUADS * GROUP)
    scale = np.where(np.arange(P) // (P // 8) % 2 == 0, 1.0, 1.0 / LANES).astype(np.float32).reshape(P, 1)
    conv_w = v["L0_conv_conv_w"][:, :, 0, 0]
    out_w = v["L1_conv_W"][:, :, 0, 0]
    return {
        "x": np.ascontiguousarray(v["x"]),
        "w_gated": blocks(conv_w[:, :C]),
        "w_plain": blocks(conv_w[:, C:]),
        "conv_b": tile(v["L0_conv_conv_b"]),
        "w_att": attention_blocks(v["L0_conv_convout_w"]),
        "att_b": tile(v["L0_conv_convout_b"]),
        "mlp_w": tile(v["L0_conv_mlp_w"]),
        "mlp_b": tile(v["L0_conv_mlp_b"]),
        "w1": np.ascontiguousarray(np.stack([blocks(out_w[:, C * k:C * (k + 1)]) for k in range(5)], axis=1)),
        "b1": tile(v["L1_conv_b"]),
        "same_group": same,
        "eye": np.eye(P, dtype=np.float32),
        "map_scale": scale,
    }


def kernel(**inputs):
    import concourse.bacc as bacc
    from concourse.bass_utils import run_bass_kernel_spmd

    arrays = layout({k: np.asarray(a) for k, a in inputs.items()})
    nc = bacc.Bacc("TRN2", target_bir_lowering=False, num_devices=1)
    args = {k: nc.dram_tensor(f"in_{k}", a.shape, mybir.dt.from_np(a.dtype), kind="ExternalInput").ap()
            for k, a in arrays.items()}
    y = nc.dram_tensor("out_y", arrays["x"].shape, F32, kind="ExternalOutput").ap()
    build(nc, y=y, **args)
    result = run_bass_kernel_spmd(nc, [{f"in_{k}": a for k, a in arrays.items()}], core_ids=[0])
    return result.results[0]["out_y"]
```
